# Optimizing a Trainium2 kernel written in Bass

```python
import numpy as np
import jax
import jax.numpy as jnp

def _softmax(x, axis=-1):
    return jax.nn.softmax(x, axis=axis)

def _gelu(x):
    return jax.nn.gelu(x, approximate=True)

def _silu(x):
    return jax.nn.silu(x)

def _sigmoid(x):
    return jax.nn.sigmoid(x)

def _layernorm(x, axis=-1, eps=1e-05):
    m = jnp.mean(x, axis=axis, keepdims=True)
    v = jnp.var(x, axis=axis, keepdims=True)
    return (x - m) / jnp.sqrt(v + eps)

def _scatter_add(tgt, idx, src, axis=0):
    return tgt.at[idx].add(src)

def _segment_sum(src, seg, n):
    return jax.ops.segment_sum(src, seg, n)
kernel_name = 'mk_adj_resnorm_d2_adj_r2_d71191'

def setup_inputs(seed: int=0):
    np.random.seed(seed)
    _w = jnp.asarray

    def _rec_inputs():
        import jax
        import jax.numpy as jnp
        _gk = jax.random.key(seed)
        x = -0.0004776 + 1.001 * jax.random.normal(jax.random.fold_in(_gk, 1), (2048, 512), jnp.float32)
        _a = jax.random.bernoulli(jax.random.fold_in(_gk, 2), 0.000976562, (2048, 2048))
        _a = jnp.logical_or(_a, jnp.eye(2048, dtype=bool))
        _af = _a.astype(jnp.float32)
        adj = _af
        return (x, adj)
    x, adj = _rec_inputs()

    def _L0_gnn_setup():
        import jax, jax.numpy as jnp
        import numpy as np
        N, H, E, HEADS = (1500, 512, 10000, 8)
        DK = H // HEADS
        key = jax.random.key(seed)
        k1, k2, k3, k4 = jax.random.split(key, 4)
        inst_feature = jax.random.normal(k1, (N, H), dtype=jnp.float32)
        rel_pair_index = jax.random.randint(k2, (E, 2), 0, N, dtype=jnp.int64)
        agg = jnp.zeros((N, N), dtype=jnp.float32)
        agg = agg.at[rel_pair_index[:, 0], rel_pair_index[:, 1]].set(1.0)
        agg = agg.at[jnp.arange(N), jnp.arange(N)].set(1.0)
        std = float(np.sqrt(2.0 / (H + DK)))
        Wq = jax.random.normal(k3, (H, H), dtype=jnp.float32) * std
        Wk = jax.random.normal(k4, (H, H), dtype=jnp.float32) * std
        bq = jnp.zeros((H,), dtype=jnp.float32)
        bk = jnp.zeros((H,), dtype=jnp.float32)
        return {'inst_feature': inst_feature, 'aggregator_matrix': agg, 'rel_pair_index': rel_pair_index, 'Wq': Wq, 'bq': bq, 'Wk': Wk, 'bk': bk}
    _L0_gnn_all = _L0_gnn_setup()
    _L0_gnn_in = {k: v for k, v in _L0_gnn_all.items() if k in ('rel_pair_index', 'Wq', 'bq', 'Wk', 'bk')}
    del _L0_gnn_all

    def _L1_gnn_setup():
        import jax, jax.numpy as jnp
        import numpy as np
        N = 4096
        D = 512

        def adjacent_mat(adj):
            adj = adj + jnp.eye(adj.shape[0], dtype=adj.dtype)
            deg = jnp.sum(adj, axis=1)
            dinv = jnp.where(deg > 0, deg ** (-0.5), 0.0).astype(adj.dtype)
            return dinv[:, None] * adj * dinv[None, :]
        key = jax.random.key(seed)
        k1, k2 = jax.random.split(key)
        x = jax.random.normal(k1, (N, D), dtype=jnp.float32)
        Coefficient2 = 1e-08 * jnp.ones((N, N), dtype=jnp.float32)
        A = jax.random.uniform(k2, (N, N), dtype=jnp.float32)
        return {'x': x, 'Coefficient2': Coefficient2, 'A': A}
    _L1_gnn_all = _L1_gnn_setup()
    _L1_gnn_in = {k: v for k, v in _L1_gnn_all.items() if k in ()}
    del _L1_gnn_all
    return {'x': x, 'adj': adj, 'L0_gnn_rel_pair_index': _L0_gnn_in['rel_pair_index'], 'L0_gnn_Wq': _L0_gnn_in['Wq'], 'L0_gnn_bq': _L0_gnn_in['bq'], 'L0_gnn_Wk': _L0_gnn_in['Wk'], 'L0_gnn_bk': _L0_gnn_in['bk']}

def reference(x, adj, L0_gnn_rel_pair_index, L0_gnn_Wq, L0_gnn_bq, L0_gnn_Wk, L0_gnn_bk):
    import jax
    import jax.numpy as jnp

    def _L0_gnn_ref(inst_feature, aggregator_matrix, rel_pair_index, Wq, bq, Wk, bk):
        import jax, jax.numpy as jnp
        import numpy as np
        N, H, E, HEADS = (1500, 512, 10000, 8)
        DK = H // HEADS
        n = inst_feature.shape[0]
        sub = rel_pair_index[:, 0]
        obj = rel_pair_index[:, 1]
        q = (inst_feature[sub] @ Wq.T + bq).reshape(-1, HEADS, DK)
        k = (inst_feature[obj] @ Wk.T + bk).reshape(-1, HEADS, DK)
        att = ((q * k).sum(-1) / np.sqrt(DK)).T.astype(inst_feature.dtype)
        scores = jnp.zeros((HEADS, n, n), dtype=inst_feature.dtype)
        scores = scores.at[:, sub, obj].set(att)
        mask = (1.0 - aggregator_matrix).astype(bool)
        scores = jnp.where(mask[None], -jnp.inf, scores)
        di = jnp.arange(n)
        scores = scores.at[:, di, di].set(1e-07)
        attn = jax.nn.softmax(scores, axis=2)
        aggregator_factor = attn.sum(axis=0) / HEADS
        return aggregator_factor @ inst_feature

    def _L1_gnn_ref(x, Coefficient2, A):
        import jax, jax.numpy as jnp
        import numpy as np
        N = 4096
        D = 512

        def adjacent_mat(adj):
            adj = adj + jnp.eye(adj.shape[0], dtype=adj.dtype)
            deg = jnp.sum(adj, axis=1)
            dinv = jnp.where(deg > 0, deg ** (-0.5), 0.0).astype(adj.dtype)
            return dinv[:, None] * adj * dinv[None, :]
        A_c = jax.lax.stop_gradient(A)
        adj = adjacent_mat((A_c + A_c.T) * 0.5)
        y = Coefficient2 @ adj
        y = y @ x
        return y
    x = _layernorm(x + _L0_gnn_ref(x, adj, L0_gnn_rel_pair_index, L0_gnn_Wq, L0_gnn_bq, L0_gnn_Wk, L0_gnn_bk), axis=-1)
    x = _layernorm(x + _L1_gnn_ref(x, adj, adj), axis=-1)
    return x

_drawn_inputs = setup_inputs


def setup_inputs(seed=0):
    import zlib

    import numpy as np

    out = dict(_drawn_inputs(seed))
    spreads = {'L0_gnn_bq': (0.0, 2.0), 'L0_gnn_bk': (0.0, 2.0)}
    factors = {'L0_gnn_Wq': 200.0, 'L0_gnn_Wk': 200.0}
    for name, (base, spread) in spreads.items():
        noise = np.random.default_rng([zlib.crc32(name.encode()), seed]).standard_normal(out[name].shape)
        drawn = base * np.exp(spread * noise) if base else spread * noise
        out[name] = jnp.asarray(drawn.astype(out[name].dtype))
    for name, factor in factors.items():
        out[name] = (out[name] * factor).astype(out[name].dtype)
    return out
```

```python
from contextlib import ExitStack

import concourse.bass as bass
from concourse import mybir

P = 128
F32 = mybir.dt.float32
BF16 = mybir.dt.bfloat16
F16 = mybir.dt.float16
F8 = mybir.dt.float8e4
I32 = mybir.dt.int32
U32 = mybir.dt.uint32
ALU = mybir.AluOpType
ACT = mybir.ActivationFunctionType
AX = mybir.AxisListType.X

HEADS = 8
SELF_SCORE = 1e-07
LN_EPS = 1e-05
BIG = 3.0e38
U_SCALE = 64.0
V_SCALE = 32.0


def gnn_residual_kernel(nc, x, adj, pairs, wq, bq, wk, bk, out):
    N, D = x.shape
    E = pairs.shape[0]
    NT = N // P
    DC = D // P
    DK = D // HEADS
    EP = 125
    EC = E // EP
    assert EP * EC == E and NT == 16 and DC == 4
    KOUT = 6

    adj_flat = adj.rearrange("a b -> (a b)").rearrange("(n o) -> n o", o=1)
    x_tiles = x.rearrange("(t p) d -> p t d", p=P)
    out_tiles = out.rearrange("(t p) d -> p t d", p=P)

    with ExitStack() as ctx:
        def sb(name, shape, dt):
            return ctx.enter_context(nc.sbuf_tensor(name, shape, dt))

        def sem(name):
            return ctx.enter_context(nc.semaphore(name))

        bank = ctx.enter_context(nc.psum_tensor("bank", [P, 8, 512], F32))
        at = sb("at", [P, NT, N], F8)
        sym = sb("sym", [P, NT, N], F8)
        xs = sb("xs", [P, 3, NT * D], BF16)
        g = sb("g", [P, NT, D], F32)
        stage = sb("stage", [P, 2, N], F32)
        arow = sb("arow", [P, 2, N], BF16)
        scratch = sb("scratch", [P, 2048], F32)
        wt = sb("wt", [P, 2, DC, D], F32)
        xi = sb("xi", [P, D], F32)
        xj = sb("xj", [P, D], F32)
        bias = sb("bias", [33, D], F32)
        ones = sb("ones", [P, P], F32)
        iota = sb("iota", [P, P + 1], F32)
        ident = sb("ident", [P, P], F32)
        identb = sb("identb", [P, P], BF16)
        ident2 = sb("ident2", [P, P], BF16)
        pair_f = sb("pair_f", [P, EC, 2], F32)
        pair_h = sb("pair_h", [P, EC, 3], F16)
        flat = sb("flat", [P, EC], I32)
        adj_e = sb("adj_e", [P, EC], F32)
        live = sb("live", [P, EC], F32)
        order = sb("order", [P, EC], F32)
        e_sm = sb("e_sm", [P, 48], F32)
        e_idx = sb("e_idx", [P, 2], I32)
        n_live = sb("n_live", [P, 1], I32)
        same_row = sb("same_row", [P, P], F32)
        tmp = sb("tmp", [P, P], F32)
        junk = sb("junk", [P, P], BF16)
        other_row = sb("other_row", [P, P], F32)
        before = other_row
        iota_i = xi[:, 0:P + 1].bitcast(I32)
        pair_i = xj[:, 0:2 * EC].bitcast(I32).rearrange("p (k c) -> p k c", c=2)
        score = sb("score", [P, HEADS], F32)
        args = sb("args", [P, 3, HEADS], F32)
        exps = sb("exps", [P, 3, HEADS], F32)
        pw = sb("pw", [P, HEADS + 1], F32)
        zz = sb("zz", [P, 4, HEADS], F32)
        trow = sb("trow", [P, 4], F32)
        row_sum = sb("row_sum", [P, NT], F32)
        diag = sb("diag", [P, NT], F32)
        deg = sb("deg", [P, NT], F32)
        col_part = sb("col_part", [P, NT, NT], F32)
        rt = sb("rt", [P, 8, NT], F32)
        stats = sb("stats", [P, 2, 6], F32)
        mv = sb("mv", [P, 4, 8], F32)

        I_, J_, V_, IV, FV, EMPTY, CNT, DG, MULT, SAME, ROWC, W1, W2, W3, TOT = range(15)
        ec = lambda k: e_sm[:, k:k + 1]
        ALPHA, BETA, SDINV, SCALE_V, T1, T2, T3 = range(7)

        xpart = lambda k, t: xs[:, k, t * D:(t + 1) * D]
        xs16 = xs[:].bitcast(F16)
        u_hi = lambda t: xs16[:, 0, t * D:(t + 1) * D]
        u_lo = lambda t: xs16[:, 1, t * D:(t + 1) * D]
        v_hi = lambda t: xs16[:, 2, t * D:(t + 1) * D]
        st16 = stage[:].rearrange("p a b -> p (a b)").bitcast(F16)
        v_lo = lambda t: st16[:, t * D:(t + 1) * D]
        xre = arow[:].rearrange("p a b -> p (a b)").bitcast(F32)
        NXR = 4
        x_again = lambda t: xre[:, (t % NXR) * D:(t % NXR + 1) * D]
        w_raw = scratch[:, 0:DC * D].rearrange("p (c d) -> p c d", c=DC)
        wt_flat = wt[:].rearrange("p a c d -> p (a c d)")
        onehot = wt_flat[:, 0:EC * P // 4].bitcast(F8).rearrange("p (k m) -> p k m", m=P)
        adj_rows = wt_flat[:, N:2 * N]
        xT = scratch[:, 0:2 * D].rearrange("p (a c e) -> p a c e", a=2, c=DC)
        edge_row = wt_flat[:, 0:N]
        masked = xT.rearrange("p a c e -> p (a c) e")
        tp = lambda I: bank[:, 2 * (I % 2):2 * (I % 2) + 2, :].rearrange("p a b -> p (a b)").bitcast(BF16)
        blk = lambda t: slice(t * P, (t + 1) * P)

        xs32 = xs[:].rearrange("p k c -> p (k c)").bitcast(F32)
        kT = xs32[:, 0:DC * N].rearrange("p (c j) -> p c j", c=DC)
        pair_mask = xs32[:, DC * N:(DC + 1) * N]
        floor = xs32[:, (DC + 1) * N:(DC + 2) * N]
        d_score = stage[:, 0, :]
        factor = stage[:, 1, :]
        fT = xre
        v_stage = scratch[:].rearrange("p (t d) -> p t d", t=4)
        gwT = wt_flat[:, 0:N].rearrange("p (c d) -> p c d", c=DC)
        gw_raw = wt_flat[:, N:2 * N].rearrange("p (c d) -> p c d", c=DC)
        qT = wt_flat[:, N:N + D].rearrange("p (c i) -> p c i", c=DC)
        row_hot = wt_flat[:, N + D:N + D + P // 2].bitcast(BF16)
        col_hot = wt_flat[:, N + 2 * D:N + 2 * D + N // 2].bitcast(BF16)
        gx = xj
        gxT = xi[:].rearrange("p (c e) -> p c e", c=DC)

        a_in = [sem("a_in0"), sem("a_in1")]
        x_in = [sem(f"x_in{b}") for b in range(4)]
        pairs_in = sem("pairs_in")
        w_in = sem("w_in")
        b_in = sem("b_in")
        iota_set = sem("iota_set")
        consts = sem("consts")
        flat_ready = sem("flat_ready")
        adj_e_in = sem("adj_e_in")
        cast_done = sem("cast_done")
        hi_done = sem("hi_done")
        res1_done = sem("res1_done")
        mid_done = sem("mid_done")
        lo_done = sem("lo_done")
        tr_done = sem("tr_done")
        at_dve = sem("at_dve")
        at_act = sem("at_act")
        cols_summed = sem("cols_summed")
        arow_read = sem("arow_read")
        g_mm = sem("g_mm")
        g_out = sem("g_out")
        w_tr = sem("w_tr")
        w_out = sem("w_out")
        chain = sem("chain")
        row_live = sem("row_live")
        prefix_mm = sem("prefix_mm")
        onehot_set = sem("onehot_set")
        compact_mm = sem("compact_mm")
        edge_idx = sem("edge_idx")
        x_edges_in = sem("x_edges_in")
        rows_in = sem("rows_in")
        bc_rhs = sem("bc_rhs")
        bc_mm = sem("bc_mm")
        xt_tr = sem("xt_tr")
        xt_out = sem("xt_out")
        bc_read = sem("bc_read")
        qk_mm = sem("qk_mm")
        score_rhs = sem("score_rhs")
        score_mm = sem("score_mm")
        args_set = sem("args_set")
        exp_done = sem("exp_done")
        pw_set = sem("pw_set")
        z_mm = sem("z_mm")
        table_rhs = sem("table_rhs")
        table_mm = sem("table_mm")
        xr_in = [sem(f"xr_in{k}") for k in range(NXR)]
        corr_mm = sem("corr_mm")
        deg_set = sem("deg_set")
        deg_root = sem("deg_root")
        var1_set = sem("var1_set")
        root1 = sem("root1")
        var2_set = sem("var2_set")
        root2 = sem("root2")
        x1_pre = sem("x1_pre")
        x1_done = sem("x1_done")
        uh_done = sem("uh_done")
        ul_done = sem("ul_done")
        z1_mm = sem("z1_mm")
        vh_done = sem("vh_done")
        vl_done = sem("vl_done")
        y_mm = sem("y_mm")
        y_read = sem("y_read")
        fin_pre = sem("fin_pre")
        fin = sem("fin")
        out_done = sem("out_done")
        gen_start = sem("gen_start")
        gen_w_in = sem("gen_w_in")
        gen_w_tr = sem("gen_w_tr")
        gen_w_out = sem("gen_w_out")
        gen_x_in = sem("gen_x_in")
        gen_x_tr = sem("gen_x_tr")
        gen_x_out = sem("gen_x_out")
        gen_p_mm = sem("gen_p_mm")
        gen_k_out = sem("gen_k_out")
        gen_q_out = sem("gen_q_out")
        gen_a_in = sem("gen_a_in")
        gen_hot = sem("gen_hot")
        gen_pair_mm = sem("gen_pair_mm")
        gen_masks = sem("gen_masks")
        gen_s_mm = sem("gen_s_mm")
        gen_s_read = sem("gen_s_read")
        gen_max = sem("gen_max")
        gen_exp = sem("gen_exp")
        gen_factor = sem("gen_factor")
        gen_f_tr = sem("gen_f_tr")
        gen_f_out = sem("gen_f_out")
        gen_v_in = sem("gen_v_in")
        gen_v_mm = sem("gen_v_mm")
        gen_row = sem("gen_row")
        gen_done = sem("gen_done")
        gen_step = sem("gen_step")

        block = ctx.enter_context(nc.Block())

        @block.sync
        def _(sp):
            def general_loads(sp):
                def load_w(w, n):
                    sp.dma_start(gw_raw, w.rearrange("(c p) d -> p c d", p=P)).then_inc(gen_w_in, 16)
                    sp.wait_ge(gen_w_tr, n)

                sp.wait_ge(gen_start, 1)
                load_w(wk, 1)
                with sp.Fori(0, NT) as J:
                    sp.wait_ge(gen_k_out, J + 1)
                    sp.dma_start(gx[:], x[bass.ds(J * P, P), :]).then_inc(gen_x_in, 16)
                sp.wait_ge(gen_k_out, NT + 1)
                load_w(wq, 2)
                with sp.Fori(0, NT) as I:
                    sp.wait_ge(gen_row, I + 1)
                    sp.dma_start(gx[:], x[bass.ds(I * P, P), :]).then_inc(gen_x_in, 16)
                    sp.dma_start(fT, adj[bass.ds(I * P, P), :]).then_inc(gen_a_in, 16)
                    for q in range(4):
                        sp.wait_ge(gen_v_mm, I * 4 + (q + 1))
                        sp.dma_start(v_stage, x_tiles[:, 4 * q:4 * q + 4, :]).then_inc(gen_v_in, 16)
                sp.wait_ge(gen_done, 1)

            sp.dma_start(pair_i[0:EP], pairs.rearrange("(p k) c -> p k c", p=EP)).then_inc(pairs_in, 16)

            def load_rows(I):
                if I >= 2:
                    sp.wait_ge(cast_done, I - 1)
                sp.dma_start(stage[:, I % 2, :], adj[blk(I), :]).then_inc(a_in[I % 2], 16)

            load_rows(0)
            for b in range(4):
                sp.dma_start(g[:, 4 * b:4 * b + 4, :], x_tiles[:, 4 * b:4 * b + 4, :]).then_inc(x_in[b], 16)
                if b == 1:
                    load_rows(1)
            sp.dma_start(w_raw, wq.rearrange("(c p) d -> p c d", p=P)).then_inc(w_in, 16)
            sp.dma_start(bias[0:1, :], bq.rearrange("(a d) -> a d", a=1)).then_inc(b_in, 16)
            sp.dma_start(bias[32:33, :], bk.rearrange("(a d) -> a d", a=1)).then_inc(b_in, 16)
            for I in range(2, NT):
                load_rows(I)
            sp.wait_ge(w_tr, 4)
            sp.dma_start(w_raw, wk.rearrange("(c p) d -> p c d", p=P)).then_inc(w_in, 16)
            sp.wait_ge(onehot_set, 1)
            with sp.If(sp.value_load(n_live[0:1, 0:1]) > P):
                general_loads(sp)
            for t in range(NT):
                if t == 0:
                    sp.wait_ge(tr_done, NT)
                    sp.wait_ge(arow_read, NT)
                if t >= NXR:
                    sp.wait_ge(x1_pre, t - NXR + 1)
                sp.dma_start(x_again(t), x_tiles[:, t, :]).then_inc(xr_in[t % NXR], 16)
            for t in range(NT):
                sp.wait_ge(fin, t + 1)
                sp.dma_start(out_tiles[:, t, :], g[:, t, :]).then_inc(out_done, 16)
            sp.wait_ge(out_done, 16 * NT)

        @block.gpsimd
        def _(pool):
            pool.iota(iota_i[:, 0:P], [[1, P]], base=1, channel_multiplier=0).then_inc(iota_set, 1)
            pool.iota(iota_i[:, P:P + 1], [[1, 1]], base=1, channel_multiplier=1).then_inc(iota_set, 1)
            pool.wait_ge(flat_ready, 1)
            for k in range(EC):
                pool.indirect_dma_start(adj_e[0:EP, k:k + 1], None, adj_flat,
                                        bass.IndirectOffsetOnAxis(ap=flat[0:EP, k:k + 1].bitcast(U32), axis=0),
                                        ).then_inc(adj_e_in, 16)
            pool.wait_ge(edge_idx, 1)
            for n, (dst, src) in enumerate(((xi, x), (xj, x))):
                pool.indirect_dma_start(dst[:], None, src,
                                        bass.IndirectOffsetOnAxis(ap=e_idx[:, n:n + 1].bitcast(U32), axis=0),
                                        ).then_inc(x_edges_in, 16)
            pool.wait_ge(qk_mm, 1)
            pool.indirect_dma_start(adj_rows, None, adj,
                                    bass.IndirectOffsetOnAxis(ap=e_idx[:, 0:1].bitcast(U32), axis=0),
                                    ).then_inc(rows_in, 16)

        @block.tensor
        def _(pe):
            def transposes(I):
                pe.wait_ge(cast_done, I + 1)
                if I >= 2:
                    pe.wait_ge(at_dve, I - 1)
                    pe.wait_ge(cols_summed, I - 1)
                    pe.wait_ge(at_act, I - 1)
                for J in range(NT):
                    last = pe.transpose(tp(I)[:, blk(J)], arow[:, I % 2, blk(J)], identb[:])
                last.then_inc(tr_done, 1)

            def adj_x(I):
                pe.wait_ge(at_dve, I + 1)
                pe.wait_ge(at_act, I + 1)
                if I >= 2:
                    pe.wait_ge(g_out, I - 1)
                for J in range(NT):
                    if I == 0 and J % 4 == 0:
                        pe.wait_ge(hi_done, J // 4 + 1)
                        pe.wait_ge(mid_done, J // 4 + 1)
                        pe.wait_ge(lo_done, J // 4 + 1)
                    for k in range(3):
                        last = pe.matmul(bank[:, 4 + I % 2, :], at[:, J, blk(I)], xpart(k, J),
                                         start=(J == 0 and k == 0), stop=(J == NT - 1 and k == 2))
                last.then_inc(g_mm, 1)

            def w_transposes(n):
                pe.wait_ge(w_in, 16 * (n // 2 + 1))
                if n == 0:
                    pe.wait_ge(bc_read, 1)
                for c in range(2):
                    if n:
                        pe.wait_ge(w_out, 2 * n + c - 1)
                    for o in range(DC):
                        last = pe.transpose(bank[:, 6 + c, blk(o)], w_raw[:, o, blk(2 * (n % 2) + c)], ident[:])
                    last.then_inc(w_tr, 1)

            def edge_prefix():
                pe.wait_ge(row_live, 1)
                pe.matmul(bank[0:EP, 6, 0:1], before[0:EP, 0:EP], e_sm[0:EP, TOT:TOT + 1], start=True, stop=True)
                pe.matmul(bank[:, 6, 1:2], ones[0:EP, :], e_sm[0:EP, TOT:TOT + 1],
                          start=True, stop=True).then_inc(prefix_mm, 1)

            def edge_compact():
                pe.wait_ge(onehot_set, 1)
                for k in range(EC):
                    last = pe.matmul(bank[:, 7, 0:3], onehot[0:EP, k, :], pair_h[0:EP, k, :],
                                     start=(k == 0), stop=(k == EC - 1))
                last.then_inc(compact_mm, 1)

            def edge_broadcast():
                pe.wait_ge(bc_rhs, 1)
                pe.matmul(bank[:, 6, 0:P], ones[:], tmp[:], start=True, stop=True)
                pe.matmul(bank[:, 6, P:2 * P], ones[:], other_row[:], start=True, stop=True).then_inc(bc_mm, 1)

            def edge_x_transposes():
                pe.wait_ge(x_edges_in, 32)
                pe.wait_ge(w_out, 8)
                for n, src in enumerate((xi, xj)):
                    for c in range(DC):
                        last = pe.transpose(bank[:, 6 + n, blk(c)], src[:, blk(c)], ident[:])
                last.then_inc(xt_tr, 1)

            def edge_project():
                pe.wait_ge(xt_out, 2)
                pe.wait_ge(b_in, 32)
                for n in range(2):
                    for c in range(DC):
                        pe.matmul(bank[:, 6 + n, :], xT[:, n, c, :], wt[:, n, c, :], start=(c == 0), stop=False)
                    last = pe.matmul(bank[:, 6 + n, :], ones[32 * n:32 * n + 1, :], bias[32 * n:32 * n + 1, :], start=False, stop=True)
                last.then_inc(qk_mm, 1)

            def edge_score_rows():
                pe.wait_ge(score_rhs, 1)
                for n in range(2):
                    last = pe.matmul(bank[:, 6 + n, :], ones[:],
                                     xT[:, n, :, :].rearrange("p c e -> p (c e)"), start=True, stop=True)
                last.then_inc(score_mm, 1)

            def edge_sums():
                pe.wait_ge(pw_set, 1)
                pe.matmul(bank[:, 6, 0:HEADS + 1], same_row[:], pw[:], start=True, stop=True).then_inc(z_mm, 1)

            def edge_table():
                pe.wait_ge(table_rhs, 1)
                for t in range(NT):
                    last = pe.matmul(bank[:, 7, 4 * t:4 * t + 3], edge_row[:, blk(t)], trow[:, 0:3],
                                     start=True, stop=True)
                last.then_inc(table_mm, 1)

            pe.wait_ge(consts, 1)
            transposes(0)
            transposes(1)
            for I in range(NT):
                adj_x(I)
                if I + 2 < NT:
                    transposes(I + 2)
                if I == 7:
                    edge_prefix()
                if I == 8:
                    edge_compact()
                if I == 9:
                    edge_broadcast()
                if I in (10, 11):
                    w_transposes(2 * (I - 10))
                    w_transposes(2 * (I - 10) + 1)
                if I == 12:
                    edge_x_transposes()
                    edge_project()
                if I == 13:
                    edge_score_rows()
                if I == 14:
                    edge_sums()
            edge_table()

            def general_products(pe):
                def w_transposed(n):
                    pe.wait_ge(gen_w_in, 16 * n)
                    for c in range(DC):
                        for o in range(DC):
                            last = pe.transpose(bank[:, c, blk(o)], gw_raw[:, o, blk(c)], ident[:])
                    last.then_inc(gen_w_tr, 1)
                    pe.wait_ge(gen_w_out, n)

                def project(n, bias_row):
                    pe.wait_ge(gen_x_in, n * 16)
                    for c in range(DC):
                        last = pe.transpose(bank[:, 0, blk(c)], gx[:, blk(c)], ident[:])
                    last.then_inc(gen_x_tr, 1)
                    pe.wait_ge(gen_x_out, n)
                    for o in range(DC):
                        for c in range(DC):
                            pe.matmul(bank[:, 1, blk(o)], gwT[:, c, blk(o)], gxT[:, c, :], start=(c == 0), stop=False)
                        last = pe.matmul(bank[:, 1, blk(o)], bias[bias_row:bias_row + 1, blk(o)],
                                         ones[bias_row:bias_row + 1, :], start=False, stop=True)
                    last.then_inc(gen_p_mm, 1)

                def pair_product(n, start, stop):
                    pe.wait_ge(gen_hot, n)
                    for c in range(4):
                        last = pe.matmul(bank[:, 2 + c, :], row_hot[0:EP, :], col_hot[0:EP, c * 512:(c + 1) * 512],
                                         start=start, stop=stop)
                    last.then_inc(gen_pair_mm, 1)

                pe.wait_ge(gen_start, 1)
                pe.wait_ge(g_out, NT)
                w_transposed(1)
                with pe.Fori(0, NT) as J:
                    pe.wait_ge(gen_k_out, J + 1)
                    project(J + 1, 32)
                pe.wait_ge(gen_k_out, NT + 1)
                w_transposed(2)
                pe.sem_inc(gen_v_mm, 1)
                with pe.Fori(0, NT) as I:
                    pe.wait_ge(gen_row, I + 1)
                    project(I + (NT + 1), 0)
                    pair_product(I * EC + 1, True, False)
                    with pe.Fori(1, EC - 1) as k:
                        pair_product(I * EC + k + 1, False, False)
                    pair_product(I * EC + EC, False, True)
                    pe.wait_ge(gen_q_out, I + 1)
                    pe.wait_ge(gen_masks, I + 1)
                    for h in range(HEADS):
                        if h:
                            pe.wait_ge(gen_s_read, I * HEADS + h)
                        half = slice(DK * (h % 2), DK * (h % 2) + DK)
                        for c in range(4):
                            last = pe.matmul(bank[:, 2 + c, :], qT[half, h // 2, :],
                                             kT[half, h // 2, c * 512:(c + 1) * 512], start=True, stop=True)
                        last.then_inc(gen_s_mm, 1)
                    pe.wait_ge(gen_factor, I + 1)
                    for J in range(NT):
                        last = pe.transpose(bank[:, 2 + J // 4, blk(J % 4)], factor[:, blk(J)], ident[:])
                    last.then_inc(gen_f_tr, 1)
                    pe.wait_ge(gen_f_out, I + 1)
                    for q in range(4):
                        pe.wait_ge(gen_v_in, I * 64 + 16 * (q + 1))
                        for r in range(4):
                            J = 4 * q + r
                            last = pe.matmul(bank[:, 6, :], fT[:, blk(J)], v_stage[:, r, :],
                                             start=(J == 0), stop=(J == NT - 1))
                        last.then_inc(gen_v_mm, 1)
                pe.wait_ge(gen_done, 1)

            with pe.If(pe.value_load(n_live[0:1, 0:1]) > P):
                general_products(pe)

            def correct(t):
                if t >= 2:
                    pe.wait_ge(x1_pre, t - 1)
                pe.matmul(bank[:, t % 2, :], edge_row[:, blk(t)], xi[:], start=True, stop=True).then_inc(corr_mm, 1)

            correct(0)
            correct(1)
            pe.wait_ge(g_out, NT)
            pe.wait_ge(x1_pre, 1)
            for J in range(NT):
                if J + 2 < NT:
                    correct(J + 2)
                pe.wait_ge(uh_done, J + 1)
                pe.wait_ge(ul_done, J + 1)
                for m in range(KOUT):
                    for k, u in enumerate((u_hi, u_lo)):
                        last = pe.matmul(bank[:, 2 + m, :], sym[:, J, blk(m)], u(J),
                                         start=(J == 0 and k == 0), stop=(J == NT - 1 and k == 1))
                    if J == NT - 1:
                        last.then_inc(z1_mm, 1)

            def bank_of(n):
                return n + 2 if n < KOUT else (n - KOUT) % 8

            def free_bank(n, eng):
                if n >= KOUT + 2:
                    eng.wait_ge(vl_done, n - 8 + 1 if n - 8 < NT else NT)
                if n >= NT + 8:
                    eng.wait_ge(y_read, n - NT - 8 + 1)

            for n in range(KOUT, NT):
                free_bank(n, pe)
                for J in range(NT):
                    for k, u in enumerate((u_hi, u_lo)):
                        last = pe.matmul(bank[:, bank_of(n), :], sym[:, J, blk(n)], u(J),
                                         start=(J == 0 and k == 0), stop=(J == NT - 1 and k == 1))
                last.then_inc(z1_mm, 1)

            def adj_v(I, J0, J1):
                for J in range(J0, J1):
                    pe.wait_ge(vh_done, J + 1)
                    pe.wait_ge(vl_done, J + 1)
                    for k, v in enumerate((v_hi, v_lo)):
                        last = pe.matmul(bank[:, bank_of(NT + I), :], at[:, J, blk(I)], v(J),
                                         start=(J == 0 and k == 0), stop=(J == NT - 1 and k == 1))
                return last

            free_bank(NT, pe)
            adj_v(0, 0, NT - 1)
            free_bank(NT + 1, pe)
            adj_v(1, 0, NT - 1)
            adj_v(0, NT - 1, NT).then_inc(y_mm, 1)
            adj_v(1, NT - 1, NT).then_inc(y_mm, 1)
            for I in range(2, NT):
                free_bank(NT + I, pe)
                adj_v(I, 0, NT).then_inc(y_mm, 1)

        @block.scalar
        def _(act):
            def cast_rows(I):
                act.wait_ge(a_in[I % 2], 16 * (I // 2 + 1))
                if I >= 2:
                    act.wait_ge(tr_done, I - 1)
                    act.wait_ge(arow_read, I - 1)
                act.activation(arow[:, I % 2, :], stage[:, I % 2, :], ACT.Copy,
                               accum_out=row_sum[:, I:I + 1]).then_inc(cast_done, 1)

            def save_at(I):
                act.wait_ge(tr_done, I + 1)
                act.copy(at[:, NT // 2:NT, blk(I)],
                         tp(I)[:, N // 2:N].rearrange("p (j i) -> p j i", i=P), saturate=False).then_inc(at_act, 1)

            def split_x(b):
                cols = slice(4 * b * D, (4 * b + 4) * D)
                src = g[:, 4 * b:4 * b + 4, :].rearrange("p t d -> p (t d)")
                act.wait_ge(x_in[b], 16)
                act.copy(xs[:, 0, cols], src).then_inc(hi_done, 1)

            def split_x_mid(b):
                cols = slice(4 * b * D, (4 * b + 4) * D)
                src = g[:, 4 * b:4 * b + 4, :].rearrange("p t d -> p (t d)")
                act.wait_ge(res1_done, b + 1)
                act.copy(xs[:, 1, cols], src).then_inc(mid_done, 1)

            cast_rows(0)
            split_x(0)
            save_at(0)
            split_x(1)
            split_x_mid(0)
            cast_rows(1)
            split_x(2)
            split_x_mid(1)
            save_at(1)
            split_x(3)
            split_x_mid(2)
            split_x_mid(3)
            cast_rows(2)
            for I in range(NT):
                if I + 2 < NT:
                    save_at(I + 2)
                if I + 3 < NT:
                    cast_rows(I + 3)
                act.wait_ge(g_mm, I + 1)
                if I == 0:
                    act.wait_ge(lo_done, 4)
                act.copy(g[:, I, :], bank[:, 4 + I % 2, :]).then_inc(g_out, 1)
                if I in (10, 11):
                    for c in range(DC):
                        act.wait_ge(w_tr, DC * (I - 10) + c + 1)
                        act.copy(wt[:, I - 10, c, :], bank[:, 6 + c % 2, :]).then_inc(w_out, 1)
                if I == 12:
                    act.wait_ge(xt_tr, 1)
                    for n in range(2):
                        act.copy(xT[:, n, :, :].rearrange("p c e -> p (c e)"), bank[:, 6 + n, :]).then_inc(xt_out, 1)
                if I == 13:
                    act.wait_ge(args_set, 1)
                    act.activation(exps[:], args[:], ACT.Exp).then_inc(exp_done, 1)
            act.wait_ge(deg_set, 1)
            act.sqrt(rt[:, T3, :], deg[:]).then_inc(deg_root, 1)
            with act.If(act.value_load(n_live[0:1, 0:1]) > P):
                with act.Fori(0, NT) as I:
                    for h in range(HEADS):
                        act.wait_ge(gen_max, I * HEADS + (h + 1))
                        act.activation(d_score, d_score, ACT.Exp, bias=mv[:, 0, 1:2],
                                       accum_out=mv[:, 0, 2:3]).then_inc(gen_exp, 1)
            for t in range(NT + 1):
                if t < NT:
                    act.wait_ge(var1_set, t + 1)
                    act.sqrt(mv[:, t % 4, 3:4], mv[:, t % 4, 2:3]).then_inc(root1, 1)
                if t:
                    act.wait_ge(x1_done, t)
                    if t == 1:
                        act.wait_ge(g_mm, NT)
                    act.activation(u_hi(t - 1), g[:, t - 1, :], ACT.Copy,
                                   scale=rt[:, SDINV, t - 1:t]).then_inc(uh_done, 1)
            for t in range(NT):
                act.wait_ge(z1_mm, t + 1)
                act.activation(v_hi(t), bank[:, t + 2 if t < KOUT else (t - KOUT) % 8, :], ACT.Copy,
                               scale=rt[:, SCALE_V, t:t + 1]).then_inc(vh_done, 1)
            for t in range(NT + 1):
                if t < NT:
                    act.wait_ge(var2_set, t + 1)
                    act.sqrt(mv[:, t % 4, 3:4], mv[:, t % 4, 2:3]).then_inc(root2, 1)
                if t:
                    act.wait_ge(fin_pre, t)
                    act.activation(g[:, t - 1, :], g[:, t - 1, :], ACT.Identity, bias=mv[:, (t - 1) % 4, 5:6],
                                   scale=mv[:, (t - 1) % 4, 4:5]).then_inc(fin, 1)

        @block.vector
        def _(dve):
            links = [0]

            def link(ins):
                links[0] += 1
                ins.then_inc(chain, 1)
                dve.wait_ge(chain, links[0])

            def mark(ins):
                links[0] += 1
                ins.then_inc(chain, 1)
                return links[0]

            mark(dve.memset(ones[:], 1.0))
            mark(dve.memset(col_part[:], 0.0))
            mark(dve.memset(pair_h[:], 1.0))
            dve.wait_ge(iota_set, 2)
            link(dve.tensor_copy(iota[:], iota_i))
            link(dve.tensor_scalar(identb[:], iota[:, 0:P], iota[:, P:P + 1], None, ALU.is_equal))
            mark(dve.tensor_scalar(ident[:], iota[:, 0:P], iota[:, P:P + 1], None, ALU.is_equal))
            mark(dve.tensor_scalar(ident2[:], identb[:], 2.0, None, ALU.mult))
            dve.tensor_scalar(before[:], iota[:, 0:P], iota[:, P:P + 1], None, ALU.is_gt).then_inc(consts, 1)
            dve.wait_ge(pairs_in, 16)
            link(dve.tensor_copy(pair_f[0:EP], pair_i[0:EP]))
            dve.scalar_tensor_tensor(flat[0:EP], pair_f[0:EP, :, 0], float(N), pair_f[0:EP, :, 1],
                                     ALU.mult, ALU.add).then_inc(flat_ready, 1)
            dve.tensor_copy(pair_h[0:EP, :, 0:2], pair_f[0:EP]).then_inc(flat_ready, 1)

            def save_at(I):
                dve.wait_ge(tr_done, I + 1)
                dve.tensor_copy(at[:, 0:NT // 2, blk(I)],
                                tp(I)[:, 0:N // 2].rearrange("p (j i) -> p j i", i=P), saturate=False).then_inc(at_dve, 1)

            def column_sums(I):
                dve.tensor_reduce(col_part[:, :, I], tp(I).rearrange("p (j i) -> p j i", i=P),
                                  AX, ALU.add).then_inc(cols_summed, 1)

            def symmetrise(I):
                w = (I + 1) * P
                dve.wait_ge(cast_done, I + 1)
                dve.wait_ge(at_dve, I + 1)
                dve.wait_ge(at_act, I + 1)
                column_sums(I)
                dve.scalar_tensor_tensor(tmp_junk, arow[:, I % 2, blk(I)], 1.0, identb[:], ALU.mult, ALU.mult,
                                         accum_out=diag[:, I:I + 1])
                if I + 1 < NT:
                    mark(dve.tensor_copy(sym[:, I, w:N], arow[:, I % 2, w:N], saturate=False))
                link(dve.scalar_tensor_tensor(sym[:, I, 0:w], arow[:, I % 2, 0:w], 1.0, at[:, I, 0:w],
                                              ALU.mult, ALU.add, saturate=False))
                mark(dve.tensor_tensor(sym[:, I, blk(I)], sym[:, I, blk(I)], ident2[:], ALU.add, saturate=False)
                     ) if I else link(dve.tensor_tensor(sym[:, I, blk(I)], sym[:, I, blk(I)], ident2[:], ALU.add, saturate=False))
                if I:
                    link(dve.tensor_tensor(sym[:, 0:I, blk(I)], sym[:, 0:I, blk(I)], at[:, 0:I, blk(I)], ALU.add, saturate=False))
                dve.tensor_copy(mv[:, 0, 0:1], diag[:, I:I + 1]).then_inc(arow_read, 1)

            tmp_junk = junk[:]

            def split_x(b):
                cols = slice(4 * b * D, (4 * b + 4) * D)
                src = g[:, 4 * b:4 * b + 4, :].rearrange("p t d -> p (t d)")
                dve.wait_ge(hi_done, b + 1)
                dve.tensor_tensor(src, src, xs[:, 0, cols], ALU.subtract).then_inc(res1_done, 1)
                dve.wait_ge(mid_done, b + 1)
                dve.tensor_tensor(xs[:, 2, cols], src, xs[:, 1, cols], ALU.subtract).then_inc(lo_done, 1)

            split_x(0)
            save_at(0)
            split_x(1)
            split_x(2)
            save_at(1)
            split_x(3)
            symmetrise(0)
            symmetrise(1)

            def edge_live():
                dve.wait_ge(adj_e_in, 16 * EC)
                link(dve.tensor_tensor(order[0:EP], pair_f[0:EP, :, 0], pair_f[0:EP, :, 1], ALU.not_equal))
                link(dve.scalar_tensor_tensor(live[0:EP], adj_e[0:EP], 1.0, order[0:EP], ALU.is_equal, ALU.mult))
                dve.tensor_reduce(e_sm[0:EP, TOT:TOT + 1], live[0:EP], AX, ALU.add).then_inc(row_live, 1)

            def edge_onehot():
                dve.wait_ge(prefix_mm, 1)
                mark(dve.tensor_copy(n_live[:], bank[:, 6, 1:2]))
                link(dve.tensor_copy(e_sm[0:EP, W1:W1 + 1], bank[0:EP, 6, 0:1]))
                link(dve.tensor_tensor_scan(order[0:EP], ones[0:EP, 0:EC], live[0:EP], e_sm[0:EP, W1:W1 + 1],
                                            ALU.mult, ALU.add))
                link(dve.tensor_tensor(order[0:EP], order[0:EP], live[0:EP], ALU.mult))
                dve.tensor_tensor(onehot[0:EP], order[0:EP].rearrange("p (k o) -> p k o", o=1).broadcast_to((EP, EC, P)),
                                  iota[0:EP, 0:P].rearrange("p (o m) -> p o m", o=1).broadcast_to((EP, EC, P)),
                                  ALU.is_equal, saturate=False).then_inc(onehot_set, 1)

            def edge_list():
                dve.wait_ge(compact_mm, 1)
                link(dve.tensor_copy(e_sm[:, 0:3], bank[:, 7, 0:3]))
                dve.tensor_copy(e_idx[:], e_sm[:, 0:2]).then_inc(edge_idx, 1)
                link(dve.scalar_tensor_tensor(ec(IV), ec(I_), -1.0, ec(V_), ALU.add, ALU.add))
                mark(dve.tensor_scalar(ec(EMPTY), ec(V_), -1.0, 1.0, ALU.mult, ALU.add))
                link(dve.scalar_tensor_tensor(ec(FV), ec(I_), float(N), ec(J_), ALU.mult, ALU.add))
                link(dve.scalar_tensor_tensor(ec(FV), ec(FV), -1.0, ec(V_), ALU.add, ALU.add))
                mark(dve.tensor_scalar(tmp[:], ident[:], ec(IV), None, ALU.mult))
                dve.tensor_scalar(other_row[:], ident[:], ec(FV), None, ALU.mult).then_inc(bc_rhs, 1)

            def edge_masks():
                dve.wait_ge(bc_mm, 1)
                link(dve.tensor_scalar(same_row[:], bank[:, 6, P:2 * P], ec(FV), 0.0, ALU.is_equal, ALU.add,
                                       accum_out=ec(MULT)))
                link(dve.tensor_scalar(same_row[:], bank[:, 6, 0:P], ec(IV), 0.0, ALU.is_equal, ALU.add,
                                       accum_out=ec(SAME)))
                dve.tensor_scalar(other_row[:], same_row[:], -1.0, BIG, ALU.add, ALU.mult).then_inc(bc_read, 1)
                link(dve.reciprocal(e_sm[:, MULT:SAME + 1], e_sm[:, MULT:SAME + 1]))
                link(dve.tensor_scalar(e_sm[:, MULT:SAME + 1], e_sm[:, MULT:SAME + 1], ec(V_), None, ALU.mult))


            def edge_scores():
                dve.wait_ge(qk_mm, 1)
                link(dve.tensor_copy(xi[:], bank[:, 6, :]))
                link(dve.tensor_tensor(xi[:], xi[:], bank[:, 7, :], ALU.mult))
                link(dve.tensor_reduce(score[:], xi[:].rearrange("p (h d) -> p h d", h=HEADS), AX, ALU.add))
                link(dve.tensor_scalar(score[:], score[:], float(DK) ** -0.5, None, ALU.mult))
                dve.tensor_tensor(masked, score[:].rearrange("p (h o) -> p h o", o=1).broadcast_to((P, HEADS, P)),
                                  ident[:].rearrange("p (o m) -> p o m", o=1).broadcast_to((P, HEADS, P)),
                                  ALU.mult).then_inc(score_rhs, 1)
                link(dve.tensor_scalar(rt[:, T1, :], iota[:, 0:NT], -float(P), ec(I_), ALU.mult, ALU.add))
                link(dve.tensor_scalar(rt[:, T1, :], rt[:, T1, :], float(P) + 1.0, None, ALU.add))
                link(dve.tensor_tensor(edge_row.rearrange("p (t m) -> p t m", m=P),
                                       rt[:, T1, :].rearrange("p (t o) -> p t o", o=1).broadcast_to((P, NT, P)),
                                       iota[:, 0:P].rearrange("p (o m) -> p o m", o=1).broadcast_to((P, NT, P)),
                                       ALU.is_equal))
                dve.wait_ge(rows_in, 16)
                link(dve.tensor_reduce(ec(ROWC), adj_rows, AX, ALU.add))
                link(dve.tensor_tensor(adj_rows, adj_rows, edge_row, ALU.mult))
                link(dve.tensor_reduce(ec(DG), adj_rows, AX, ALU.add))
                link(dve.tensor_tensor(ec(CNT), ec(ROWC), ec(DG), ALU.subtract))

            def edge_max():
                dve.wait_ge(score_mm, 1)
                link(dve.tensor_tensor(masked, bank[:, 6:8, :].rearrange("p a (c e) -> p (a c) e", e=P),
                                       other_row[:].rearrange("p (o m) -> p o m", o=1).broadcast_to((P, HEADS, P)),
                                       ALU.add))
                link(dve.tensor_reduce(zz[:, 0, :], masked, AX, ALU.max))
                link(dve.tensor_scalar(args[:, 0, :], zz[:, 0, :], SELF_SCORE, -1.0, ALU.max, ALU.mult))
                mark(dve.tensor_scalar(args[:, 1, :], args[:, 0, :], SELF_SCORE, None, ALU.add))
                dve.tensor_tensor(args[:, 2, :], args[:, 0, :], score[:], ALU.add).then_inc(args_set, 1)
                dve.wait_ge(exp_done, 1)
                mark(dve.tensor_scalar(pw[:, 0:HEADS], exps[:, 2, :], ec(MULT), None, ALU.mult))
                dve.tensor_copy(pw[:, HEADS:HEADS + 1], ec(MULT)).then_inc(pw_set, 1)

            def edge_weights():
                dve.wait_ge(z_mm, 1)
                link(dve.tensor_tensor(ec(CNT), ec(CNT), bank[:, 6, HEADS:HEADS + 1], ALU.subtract))
                link(dve.scalar_tensor_tensor(zz[:, 1, :], exps[:, 0, :], ec(CNT), exps[:, 1, :], ALU.mult, ALU.add))
                link(dve.tensor_tensor(zz[:, 1, :], zz[:, 1, :], bank[:, 6, 0:HEADS], ALU.add))
                link(dve.tensor_scalar(zz[:, 1, :], zz[:, 1, :], ec(EMPTY), float(HEADS), ALU.add, ALU.mult))
                link(dve.reciprocal(zz[:, 1, :], zz[:, 1, :]))
                for n, w in enumerate((W1, W2, W3)):
                    link(dve.tensor_tensor(zz[:, 2, :], exps[:, n, :], zz[:, 1, :], ALU.mult))
                    link(dve.tensor_reduce(ec(w), zz[:, 2, :], AX, ALU.add))
                link(dve.tensor_tensor(ec(W3), ec(W3), ec(W1), ALU.subtract))
                link(dve.tensor_tensor(ec(W3), ec(W3), ec(MULT), ALU.mult))
                mark(dve.tensor_scalar(xi[:], xj[:], ec(W3), None, ALU.mult))
                mark(dve.tensor_copy(trow[:, 0:1], ec(SAME)))
                dve.tensor_scalar(trow[:, 1:3], e_sm[:, W1:W2 + 1], ec(SAME), None, ALU.mult).then_inc(table_rhs, 1)

            def inverse_root(v, root, out, w):
                link(dve.reciprocal(out, root))
                link(dve.tensor_tensor(w, out, out, ALU.mult))
                link(dve.tensor_tensor(w, w, v, ALU.mult))
                link(dve.tensor_scalar(w, w, -0.5, 1.5, ALU.mult, ALU.add))
                link(dve.tensor_tensor(out, out, w, ALU.mult))

            def row_coefficients():
                tab = bank[:, 7, 0:4 * NT].rearrange("p (t c) -> p c t", c=4)
                em0 = float(np_exp(-SELF_SCORE))
                r = lambda k: rt[:, k, :]
                link(dve.tensor_tensor(r(T1), row_sum[:], diag[:], ALU.subtract))
                link(dve.tensor_scalar(r(T1), r(T1), em0, 1.0, ALU.mult, ALU.add))
                link(dve.reciprocal(r(T1), r(T1)))
                link(dve.tensor_reduce(r(T2), col_part[:], AX, ALU.add))
                link(dve.tensor_tensor(r(T2), r(T2), row_sum[:], ALU.add))
                link(dve.tensor_scalar(r(T2), r(T2), 0.5, 1.0, ALU.mult, ALU.add))
                dve.tensor_copy(deg[:], r(T2)).then_inc(deg_set, 1)
                dve.wait_ge(deg_root, 1)
                inverse_root(deg[:], r(T3), r(T2), r(SDINV))
                mark(dve.tensor_scalar(r(SDINV), r(T2), U_SCALE, None, ALU.mult))
                link(dve.tensor_scalar(r(SCALE_V), r(T2), 0.5 * V_SCALE / U_SCALE, None, ALU.mult))
                dve.wait_ge(table_mm, 1)
                link(dve.tensor_scalar(r(T3), tab[:, 0, :], -1.0, 1.0, ALU.mult, ALU.add))
                link(dve.tensor_tensor(r(T3), r(T3), r(T1), ALU.mult))
                link(dve.scalar_tensor_tensor(r(ALPHA), r(T3), em0, tab[:, 1, :], ALU.mult, ALU.add))
                link(dve.tensor_tensor(r(BETA), r(T3), tab[:, 2, :], ALU.add))
                link(dve.tensor_tensor(r(T3), r(ALPHA), diag[:], ALU.mult))
                link(dve.scalar_tensor_tensor(r(BETA), r(BETA), 1.0, r(T3), ALU.add, ALU.subtract))

            for I in range(NT):
                if I + 2 < NT:
                    save_at(I + 2)
                    symmetrise(I + 2)
                if I == 6:
                    edge_live()
                if I == 7:
                    edge_onehot()
                if I == 8:
                    edge_list()
                if I == 9:
                    edge_masks()
                if I == 12:
                    edge_scores()
                if I == 13:
                    edge_max()
                if I == 14:
                    edge_weights()
            row_coefficients()

            def general_path(dve):
                shift, tile_no = mv[:, 1, 0:1], mv[:, 1, 1:2]
                n_sem = [0]

                def step(ins):
                    ins.then_inc(gen_step, 1)
                    dve.wait_ge(gen_step, 1)
                    dve.sem_clear(gen_step)

                def w_out(n):
                    dve.wait_ge(gen_w_tr, n)
                    dve.tensor_copy(gwT.rearrange("p c d -> p (c d)"),
                                    bank[:, 0:4, :].rearrange("p a b -> p (a b)")).then_inc(gen_w_out, 1)

                def x_out(n):
                    dve.wait_ge(gen_x_tr, n)
                    dve.tensor_copy(xi[:], bank[:, 0, :]).then_inc(gen_x_out, 1)
                    dve.wait_ge(gen_p_mm, n)

                def hot(k, n):
                    step(dve.tensor_scalar(rt[0:EP, T1, :], iota[0:EP, 0:NT], -float(P), float(P) + 1.0,
                                           ALU.mult, ALU.add))
                    step(dve.tensor_scalar(rt[0:EP, T1, :], rt[0:EP, T1, :], pair_f[0:EP, bass.ds(k, 1), 1], None, ALU.add))
                    mark_g(dve.tensor_scalar(row_hot[0:EP, :], iota[0:EP, 0:P], shift[0:EP],
                                             pair_f[0:EP, bass.ds(k, 1), 0], ALU.add, ALU.is_equal))
                    dve.tensor_tensor(col_hot[0:EP, :].rearrange("p (t m) -> p t m", m=P),
                                      rt[0:EP, T1, :].rearrange("p (t o) -> p t o", o=1).broadcast_to((EP, NT, P)),
                                      iota[0:EP, 0:P].rearrange("p (o m) -> p o m", o=1).broadcast_to((EP, NT, P)),
                                      ALU.is_equal).then_inc(gen_hot, 1)

                def mark_g(ins):
                    pass

                dve.wait_ge(g_mm, NT)
                dve.wait_ge(g_out, NT)
                dve.memset(shift, -1.0)
                step(dve.memset(tile_no, 1.0))
                dve.sem_inc(gen_start, 1)
                w_out(1)
                dve.sem_inc(gen_k_out, 1)
                with dve.Fori(0, NT) as J:
                    x_out(J + 1)
                    dve.tensor_copy(kT[:, :, bass.ds(J * P, P)],
                                    bank[:, 1, :].rearrange("p (c e) -> p c e", c=DC)).then_inc(gen_k_out, 1)
                w_out(2)
                dve.sem_inc(gen_row, 1)
                with dve.Fori(0, NT) as I:
                    x_out(I + (NT + 1))
                    dve.tensor_copy(qT, bank[:, 1, :].rearrange("p (c e) -> p c e", c=DC)).then_inc(gen_q_out, 1)
                    hot(0, I)
                    with dve.Fori(1, EC) as k:
                        dve.wait_ge(gen_pair_mm, I * EC + k)
                        hot(k, I)
                    dve.wait_ge(gen_pair_mm, I * EC + EC)
                    step(dve.tensor_scalar(rt[:, T1, :], iota[:, 0:NT], tile_no, iota[:, P:P + 1],
                                           ALU.is_equal, ALU.mult))
                    step(dve.tensor_tensor(factor.rearrange("p (t m) -> p t m", m=P),
                                           rt[:, T1, :].rearrange("p (t o) -> p t o", o=1).broadcast_to((P, NT, P)),
                                           iota[:, 0:P].rearrange("p (o m) -> p o m", o=1).broadcast_to((P, NT, P)),
                                           ALU.is_equal))
                    step(dve.tensor_scalar(d_score, factor, -1.0, 1.0, ALU.mult, ALU.add))
                    dve.wait_ge(gen_a_in, I * 16 + 16)
                    step(dve.tensor_scalar(floor, fT, 1.0, -1.0, ALU.is_equal, ALU.add))
                    step(dve.scalar_tensor_tensor(floor, floor, BIG, d_score, ALU.mult, ALU.mult))
                    step(dve.scalar_tensor_tensor(floor, factor, SELF_SCORE, floor, ALU.mult, ALU.add))
                    dve.scalar_tensor_tensor(pair_mask, bank[:, 2:6, :].rearrange("p a b -> p (a b)"), 1.0, d_score,
                                             ALU.min, ALU.mult).then_inc(gen_masks, 1)
                    step(dve.memset(factor, 0.0))
                    for h in range(HEADS):
                        dve.wait_ge(gen_masks, I + 1)
                        dve.wait_ge(gen_s_mm, I * HEADS + (h + 1))
                        ins = dve.scalar_tensor_tensor(d_score, bank[:, 2:6, :].rearrange("p a b -> p (a b)"),
                                                       float(DK) ** -0.5, pair_mask, ALU.mult, ALU.mult)
                        ins.then_inc(gen_s_read, 1)
                        dve.wait_ge(gen_s_read, I * HEADS + (h + 1))
                        step(dve.tensor_tensor(d_score, d_score, floor, ALU.add))
                        step(dve.tensor_reduce(mv[:, 0, 0:1], d_score, AX, ALU.max))
                        dve.tensor_scalar(mv[:, 0, 1:2], mv[:, 0, 0:1], -1.0, None, ALU.mult).then_inc(gen_max, 1)
                        dve.wait_ge(gen_exp, I * HEADS + (h + 1))
                        step(dve.tensor_scalar(mv[:, 0, 3:4], mv[:, 0, 2:3], float(HEADS), None, ALU.mult))
                        step(dve.reciprocal(mv[:, 0, 3:4], mv[:, 0, 3:4]))
                        ins = dve.scalar_tensor_tensor(factor, d_score, mv[:, 0, 3:4], factor, ALU.mult, ALU.add)
                        if h < HEADS - 1:
                            step(ins)
                        else:
                            ins.then_inc(gen_factor, 1)
                    dve.wait_ge(gen_f_tr, I + 1)
                    dve.tensor_copy(fT, bank[:, 2:6, :].rearrange("p a b -> p (a b)")).then_inc(gen_f_out, 1)
                    dve.tensor_scalar(shift, shift, float(P), None, ALU.add)
                    step(dve.tensor_scalar(tile_no, tile_no, 1.0, None, ALU.add))
                    dve.wait_ge(gen_v_mm, I * 4 + 5)
                    dve.tensor_copy(g[:, bass.ds(I, 1), :], bank[:, 6:7, :]).then_inc(gen_row, 1)
                dve.memset(xi[:], 0.0)
                dve.memset(rt[:, ALPHA, :], 1.0)
                step(dve.memset(rt[:, BETA, :], 1.0))
                dve.wait_ge(gen_row, NT + 1)
                dve.sem_inc(gen_done, 1)

            with dve.If(dve.value_load(n_live[0:1, 0:1]) > P):
                general_path(dve)

            def moments(t, var_set):
                m = mv[:, t % 4, :]
                link(dve.bn_stats(stats[:, t % 2, :], g[:, t, :]))
                link(dve.bn_aggr(m[:, 0:2], stats[:, t % 2, :]))
                dve.tensor_scalar(m[:, 2:3], m[:, 1:2], LN_EPS, None, ALU.add).then_inc(var_set, 1)

            def x1_sum(t):
                dve.wait_ge(corr_mm, t + 1)
                dve.wait_ge(g_out, t + 1)
                link(dve.scalar_tensor_tensor(g[:, t, :], g[:, t, :], rt[:, ALPHA, t:t + 1], bank[:, t % 2, :],
                                              ALU.mult, ALU.add))
                dve.wait_ge(xr_in[t % NXR], 16 * (t // NXR + 1))
                dve.scalar_tensor_tensor(g[:, t, :], x_again(t), rt[:, BETA, t:t + 1], g[:, t, :],
                                         ALU.mult, ALU.add).then_inc(x1_pre, 1)
                dve.wait_ge(x1_pre, t + 1)
                moments(t, var1_set)

            def x1_normalise(t):
                m = mv[:, t % 4, :]
                dve.wait_ge(root1, t + 1)
                inverse_root(m[:, 2:3], m[:, 3:4], m[:, 4:5], m[:, 6:7])
                dve.tensor_scalar(g[:, t, :], g[:, t, :], m[:, 0:1], m[:, 4:5],
                                  ALU.subtract, ALU.mult).then_inc(x1_done, 1)

            def u_low(t):
                dve.wait_ge(x1_done, t + 1)
                dve.wait_ge(uh_done, t + 1)
                dve.scalar_tensor_tensor(u_lo(t), g[:, t, :], rt[:, SDINV, t:t + 1], u_hi(t),
                                         ALU.mult, ALU.subtract).then_inc(ul_done, 1)

            for t in range(NT + 2):
                if t < NT:
                    x1_sum(t)
                if 1 <= t <= NT:
                    x1_normalise(t - 1)
                if t >= 2:
                    u_low(t - 2)
            for t in range(NT):
                dve.wait_ge(vh_done, t + 1)
                dve.scalar_tensor_tensor(v_lo(t), bank[:, t + 2 if t < KOUT else (t - KOUT) % 8, :],
                                         rt[:, SCALE_V, t:t + 1], v_hi(t),
                                         ALU.mult, ALU.subtract).then_inc(vl_done, 1)
            for t in range(NT + 1):
                if t < NT:
                    dve.wait_ge(y_mm, t + 1)
                    n = NT + t - KOUT
                    dve.scalar_tensor_tensor(g[:, t, :], bank[:, n % 8, :], 1.0 / V_SCALE, g[:, t, :],
                                             ALU.mult, ALU.add).then_inc(y_read, 1)
                    dve.wait_ge(y_read, t + 1)
                    if t >= 4:
                        dve.wait_ge(fin, t - 3)
                    moments(t, var2_set)
                if t:
                    m = mv[:, (t - 1) % 4, :]
                    dve.wait_ge(root2, t)
                    inverse_root(m[:, 2:3], m[:, 3:4], m[:, 4:5], m[:, 6:7])
                    dve.scalar_tensor_tensor(m[:, 5:6], m[:, 0:1], -1.0, m[:, 4:5],
                                             ALU.mult, ALU.mult).then_inc(fin_pre, 1)


def np_exp(v):
    import numpy as np
    return np.exp(np.float64(v))


_INS = ['x', 'adj', 'L0_gnn_rel_pair_index', 'L0_gnn_Wq', 'L0_gnn_bq', 'L0_gnn_Wk', 'L0_gnn_bk']


def kernel(**inputs):
    import numpy as _np
    import concourse.bacc as _bacc
    from concourse import mybir as _mybir
    from concourse.bass_utils import run_bass_kernel_spmd as _run

    nc = _bacc.Bacc("TRN2", target_bir_lowering=False, num_devices=1)
    arrays, args = {}, []
    for name in _INS:
        a = _np.ascontiguousarray(inputs[name])
        arrays[f"in_{name}_dram"] = a
        args.append(nc.dram_tensor(f"in_{name}_dram", a.shape, _mybir.dt.from_np(a.dtype), kind="ExternalInput").ap())
    args.append(nc.dram_tensor("out_dram", args[0].shape, _mybir.dt.float32, kind="ExternalOutput").ap())
    gnn_residual_kernel(nc, *args)
    r = _run(nc, [arrays], core_ids=[0])
    return r.results[0]["out_dram"]
```

```python
from contextlib import ExitStack

import concourse.bass as bass
from concourse import mybir

P = 128
F32 = mybir.dt.float32
BF16 = mybir.dt.bfloat16
F16 = mybir.dt.float16
F8 = mybir.dt.float8e4
I32 = mybir.dt.int32
U32 = mybir.dt.uint32
ALU = mybir.AluOpType
ACT = mybir.ActivationFunctionType
AX = mybir.AxisListType.X

HEADS = 8
SELF_SCORE = 1e-07
LN_EPS = 1e-05
BIG = 3.0e38
U_SCALE = 64.0
V_SCALE = 32.0


def gnn_residual_kernel(nc, x, adj, pairs, wq, bq, wk, bk, out):
    N, D = x.shape
    E = pairs.shape[0]
    NT = N // P
    DC = D // P
    DK = D // HEADS
    EP = 125
    EC = E // EP
    assert EP * EC == E and NT == 16 and DC == 4
    KOUT = 5

    adj_flat = adj.rearrange("a b -> (a b)").rearrange("(n o) -> n o", o=1)
    x_tiles = x.rearrange("(t p) d -> p t d", p=P)
    out_tiles = out.rearrange("(t p) d -> p t d", p=P)

    with ExitStack() as ctx:
        def sb(name, shape, dt):
            return ctx.enter_context(nc.sbuf_tensor(name, shape, dt))

        def sem(name):
            return ctx.enter_context(nc.semaphore(name))

        bank = ctx.enter_context(nc.psum_tensor("bank", [P, 8, 512], F32))
        at = sb("at", [P, NT, N], F8)
        sym = sb("sym", [P, NT, N], F8)
        xs = sb("xs", [P, 3, NT * D], BF16)
        g = sb("g", [P, NT, D], F32)
        stage = sb("stage", [P, 2, N], F32)
        arow = sb("arow", [P, 2, N], BF16)
        scratch = sb("scratch", [P, 2048], F32)
        wt = sb("wt", [P, 2, DC, D], F32)
        xi = sb("xi", [P, D], F32)
        xj = sb("xj", [P, D], F32)
        bias = sb("bias", [33, D], F32)
        ones = sb("ones", [P, P], F32)
        iota = sb("iota", [P, P + 1], F32)
        ident = sb("ident", [P, P], F32)
        identb = sb("identb", [P, P], BF16)
        ident2 = sb("ident2", [P, P], BF16)
        pair_f = sb("pair_f", [P, EC, 2], F32)
        pair_h = sb("pair_h", [P, EC, 3], F16)
        flat = sb("flat", [P, EC], I32)
        adj_e = sb("adj_e", [P, EC], F32)
        live = sb("live", [P, EC], F32)
        order = sb("order", [P, EC], F32)
        e_sm = sb("e_sm", [P, 48], F32)
        e_idx = sb("e_idx", [P, 2], I32)
        n_live = sb("n_live", [P, 1], I32)
        same_row = sb("same_row", [P, P], F32)
        tmp = sb("tmp", [P, P], F32)
        junk = sb("junk", [P, P], BF16)
        other_row = sb("other_row", [P, P], F32)
        before = other_row
        iota_i = xi[:, 0:P + 1].bitcast(I32)
        pair_i = xj[:, 0:2 * EC].bitcast(I32).rearrange("p (k c) -> p k c", c=2)
        score = sb("score", [P, HEADS], F32)
        args = sb("args", [P, 3, HEADS], F32)
        exps = sb("exps", [P, 3, HEADS], F32)
        pw = sb("pw", [P, HEADS + 1], F32)
        zz = sb("zz", [P, 4, HEADS], F32)
        trow = sb("trow", [P, 4], F32)
        row_sum = sb("row_sum", [P, NT], F32)
        diag = sb("diag", [P, NT], F32)
        deg = sb("deg", [P, NT], F32)
        col_part = sb("col_part", [P, NT, NT], F32)
        rt = sb("rt", [P, 8, NT], F32)
        xscale = sb("xscale", [P, 8], F32)
        xscale_i = xscale[:].bitcast(I32)
        stats = sb("stats", [P, 2, 6], F32)
        mv = sb("mv", [P, 4, 8], F32)

        I_, J_, V_, IV, FV, EMPTY, CNT, DG, MULT, SAME, ROWC, W1, W2, W3, TOT = range(15)
        ec = lambda k: e_sm[:, k:k + 1]
        ALPHA, BETA, SDINV, SCALE_V, T1, T2, T3 = range(7)

        xs16 = xs[:].bitcast(F16)
        xpart = lambda k, t: xs16[:, k, t * D:(t + 1) * D]
        u_hi = lambda t: xs16[:, 0, t * D:(t + 1) * D]
        u_lo = lambda t: xs16[:, 1, t * D:(t + 1) * D]
        v_hi = lambda t: xs16[:, 2, t * D:(t + 1) * D]
        st16 = stage[:].rearrange("p a b -> p (a b)").bitcast(F16)
        v_lo = lambda t: st16[:, t * D:(t + 1) * D]
        xre = arow[:].rearrange("p a b -> p (a b)").bitcast(F32)
        NXR = 4
        x_again = lambda t: xre[:, (t % NXR) * D:(t % NXR + 1) * D]
        w_raw = scratch[:, 0:DC * D].rearrange("p (c d) -> p c d", c=DC)
        wt_flat = wt[:].rearrange("p a c d -> p (a c d)")
        spare = xs[:, 2, :].bitcast(F32)
        onehot = spare[:, 0:EC * P // 4].bitcast(F8).rearrange("p (k m) -> p k m", m=P)
        adj_rows = spare[:, 0:N]
        xT = scratch[:, 0:2 * D].rearrange("p (a c e) -> p a c e", a=2, c=DC)
        edge_row = wt_flat[:, 0:N]
        masked = xT.rearrange("p a c e -> p (a c) e")
        tp = lambda I: bank[:, 2 * (I % 2):2 * (I % 2) + 2, :].rearrange("p a b -> p (a b)").bitcast(BF16)
        bank_of = lambda n: (2, 3, 4, 5, 6, 0, 1, 7)[n % 8]
        blk = lambda t: slice(t * P, (t + 1) * P)

        xs32 = xs[:].rearrange("p k c -> p (k c)").bitcast(F32)
        kT = xs32[:, 0:DC * N].rearrange("p (c j) -> p c j", c=DC)
        pair_mask = xs32[:, DC * N:(DC + 1) * N]
        floor = xs32[:, (DC + 1) * N:(DC + 2) * N]
        d_score = stage[:, 0, :]
        factor = stage[:, 1, :]
        fT = xre
        v_stage = scratch[:].rearrange("p (t d) -> p t d", t=4)
        gwT = wt_flat[:, 0:N].rearrange("p (c d) -> p c d", c=DC)
        gw_raw = wt_flat[:, N:2 * N].rearrange("p (c d) -> p c d", c=DC)
        qT = wt_flat[:, N:N + D].rearrange("p (c i) -> p c i", c=DC)
        row_hot = wt_flat[:, N + D:N + D + P // 2].bitcast(BF16)
        col_hot = wt_flat[:, N + 2 * D:N + 2 * D + N // 2].bitcast(BF16)
        gx = xj
        gxT = xi[:].rearrange("p (c e) -> p c e", c=DC)

        a_in = [sem("a_in0"), sem("a_in1")]
        x_in = [sem(f"x_in{b}") for b in range(4)]
        pairs_in = sem("pairs_in")
        w_in = sem("w_in")
        b_in = sem("b_in")
        iota_set = sem("iota_set")
        consts = sem("consts")
        flat_ready = sem("flat_ready")
        adj_e_in = sem("adj_e_in")
        cast_done = sem("cast_done")
        max_diag = sem("max_diag")
        max_mm = sem("max_mm")
        scale_set = sem("scale_set")
        hi_done = sem("hi_done")
        lo_done = sem("lo_done")
        tr_done = sem("tr_done")
        at_act = sem("at_act")
        cols_summed = sem("cols_summed")
        arow_read = sem("arow_read")
        g_mm = sem("g_mm")
        g_out = sem("g_out")
        w_tr = sem("w_tr")
        w_out = sem("w_out")
        chain = sem("chain")
        row_live = sem("row_live")
        prefix_mm = sem("prefix_mm")
        onehot_set = sem("onehot_set")
        compact_mm = sem("compact_mm")
        edge_idx = sem("edge_idx")
        x_edges_in = sem("x_edges_in")
        rows_in = sem("rows_in")
        bc_rhs = sem("bc_rhs")
        bc_mm = sem("bc_mm")
        xt_tr = sem("xt_tr")
        xt_out = sem("xt_out")
        bc_read = sem("bc_read")
        qk_mm = sem("qk_mm")
        score_rhs = sem("score_rhs")
        score_mm = sem("score_mm")
        args_set = sem("args_set")
        exp_done = sem("exp_done")
        pw_set = sem("pw_set")
        z_mm = sem("z_mm")
        table_rhs = sem("table_rhs")
        table_mm = sem("table_mm")
        xr_in = [sem(f"xr_in{k}") for k in range(NXR)]
        corr_mm = sem("corr_mm")
        coef_set = sem("coef_set")
        deg_set = sem("deg_set")
        deg_root = sem("deg_root")
        var1_set = sem("var1_set")
        root1 = sem("root1")
        norm1_set = sem("norm1_set")
        var2_set = sem("var2_set")
        root2 = sem("root2")
        x1_pre = sem("x1_pre")
        x1_done = sem("x1_done")
        uh_done = sem("uh_done")
        ul_done = sem("ul_done")
        z1_mm = sem("z1_mm")
        vh_done = sem("vh_done")
        vl_done = sem("vl_done")
        y_mm = sem("y_mm")
        y_read = sem("y_read")
        fin_pre = sem("fin_pre")
        fin = sem("fin")
        out_done = sem("out_done")
        gen_start = sem("gen_start")
        gen_w_in = sem("gen_w_in")
        gen_w_tr = sem("gen_w_tr")
        gen_w_out = sem("gen_w_out")
        gen_x_in = sem("gen_x_in")
        gen_x_tr = sem("gen_x_tr")
        gen_x_out = sem("gen_x_out")
        gen_p_mm = sem("gen_p_mm")
        gen_k_out = sem("gen_k_out")
        gen_q_out = sem("gen_q_out")
        gen_a_in = sem("gen_a_in")
        gen_hot = sem("gen_hot")
        gen_pair_mm = sem("gen_pair_mm")
        gen_masks = sem("gen_masks")
        gen_s_mm = sem("gen_s_mm")
        gen_s_read = sem("gen_s_read")
        gen_max = sem("gen_max")
        gen_exp = sem("gen_exp")
        gen_factor = sem("gen_factor")
        gen_f_tr = sem("gen_f_tr")
        gen_f_out = sem("gen_f_out")
        gen_v_in = sem("gen_v_in")
        gen_v_mm = sem("gen_v_mm")
        gen_row = sem("gen_row")
        gen_done = sem("gen_done")
        gen_step = sem("gen_step")

        block = ctx.enter_context(nc.Block())

        @block.sync
        def _(sp):
            def general_loads(sp):
                def load_w(w, n):
                    sp.dma_start(gw_raw, w.rearrange("(c p) d -> p c d", p=P)).then_inc(gen_w_in, 16)
                    sp.wait_ge(gen_w_tr, n)

                sp.wait_ge(gen_start, 1)
                load_w(wk, 1)
                with sp.Fori(0, NT) as J:
                    sp.wait_ge(gen_k_out, J + 1)
                    sp.dma_start(gx[:], x[bass.ds(J * P, P), :]).then_inc(gen_x_in, 16)
                sp.wait_ge(gen_k_out, NT + 1)
                load_w(wq, 2)
                with sp.Fori(0, NT) as I:
                    sp.wait_ge(gen_row, I + 1)
                    sp.dma_start(gx[:], x[bass.ds(I * P, P), :]).then_inc(gen_x_in, 16)
                    sp.dma_start(fT, adj[bass.ds(I * P, P), :]).then_inc(gen_a_in, 16)
                    for q in range(4):
                        sp.wait_ge(gen_v_mm, I * 4 + (q + 1))
                        sp.dma_start(v_stage, x_tiles[:, 4 * q:4 * q + 4, :]).then_inc(gen_v_in, 16)
                sp.wait_ge(gen_done, 1)

            sp.dma_start(pair_i[0:EP], pairs.rearrange("(p k) c -> p k c", p=EP)).then_inc(pairs_in, 16)

            def load_rows(I):
                if I >= 2:
                    sp.wait_ge(cast_done, I - 1)
                sp.dma_start(stage[:, I % 2, :], adj[blk(I), :]).then_inc(a_in[I % 2], 16)

            for b in range(4):
                sp.dma_start(g[:, 4 * b:4 * b + 4, :], x_tiles[:, 4 * b:4 * b + 4, :]).then_inc(x_in[b], 16)
            load_rows(0)
            load_rows(1)
            sp.dma_start(w_raw, wq.rearrange("(c p) d -> p c d", p=P)).then_inc(w_in, 16)
            sp.dma_start(bias[0:1, :], bq.rearrange("(a d) -> a d", a=1)).then_inc(b_in, 16)
            sp.dma_start(bias[32:33, :], bk.rearrange("(a d) -> a d", a=1)).then_inc(b_in, 16)
            for I in range(2, NT):
                load_rows(I)
                if I == 6:
                    sp.wait_ge(w_tr, 4)
                    sp.dma_start(w_raw, wk.rearrange("(c p) d -> p c d", p=P)).then_inc(w_in, 16)
            sp.wait_ge(onehot_set, 1)
            with sp.If(sp.value_load(n_live[0:1, 0:1]) > P):
                general_loads(sp)
            for t in range(NT):
                if t == 0:
                    sp.wait_ge(tr_done, NT)
                    sp.wait_ge(arow_read, NT)
                if t >= NXR:
                    sp.wait_ge(x1_pre, t - NXR + 1)
                sp.dma_start(x_again(t), x_tiles[:, t, :]).then_inc(xr_in[t % NXR], 16)
            for t in range(NT):
                sp.wait_ge(fin, t + 1)
                sp.dma_start(out_tiles[:, t, :], g[:, t, :]).then_inc(out_done, 16)
            sp.wait_ge(out_done, 16 * NT)

        @block.gpsimd
        def _(pool):
            pool.iota(iota_i[:, 0:P], [[1, P]], base=1, channel_multiplier=0).then_inc(iota_set, 1)
            pool.iota(iota_i[:, P:P + 1], [[1, 1]], base=1, channel_multiplier=1).then_inc(iota_set, 1)
            pool.wait_ge(flat_ready, 1)
            for k in range(EC):
                pool.indirect_dma_start(adj_e[0:EP, k:k + 1], None, adj_flat,
                                        bass.IndirectOffsetOnAxis(ap=flat[0:EP, k:k + 1].bitcast(U32), axis=0),
                                        ).then_inc(adj_e_in, 16)
            pool.wait_ge(edge_idx, 1)
            for n, (dst, src) in enumerate(((xi, x), (xj, x))):
                pool.indirect_dma_start(dst[:], None, src,
                                        bass.IndirectOffsetOnAxis(ap=e_idx[:, n:n + 1].bitcast(U32), axis=0),
                                        ).then_inc(x_edges_in, 16)
            pool.indirect_dma_start(adj_rows, None, adj,
                                    bass.IndirectOffsetOnAxis(ap=e_idx[:, 0:1].bitcast(U32), axis=0),
                                    ).then_inc(rows_in, 16)

        @block.tensor
        def _(pe):
            def transposes(I):
                pe.wait_ge(cast_done, I + 1)
                if I >= 2:
                    pe.wait_ge(cols_summed, I - 1)
                    pe.wait_ge(at_act, I - 1)
                for J in range(NT):
                    last = pe.transpose(tp(I)[:, blk(J)], arow[:, I % 2, blk(J)], identb[:])
                last.then_inc(tr_done, 1)

            def adj_x(I, J0=0, J1=NT):
                if J0 == 0:
                    pe.wait_ge(at_act, I + 1)
                    if I >= 2:
                        pe.wait_ge(g_out, I - 1)
                for J in range(J0, J1):
                    for k in range(2):
                        last = pe.matmul(bank[:, 4 + I % 2, :], at[:, J, blk(I)], xpart(k, J),
                                         start=(J == 0 and k == 0), stop=(J == NT - 1 and k == 1))
                if J1 == NT:
                    last.then_inc(g_mm, 1)

            def w_transposes(n):
                pe.wait_ge(w_in, 16 * (n // 2 + 1))
                for c in range(2):
                    if n:
                        pe.wait_ge(w_out, 2 * n + c - 1)
                    for o in range(DC):
                        last = pe.transpose(bank[:, 6 + c, blk(o)], w_raw[:, o, blk(2 * (n % 2) + c)], ident[:])
                    last.then_inc(w_tr, 1)

            def edge_prefix():
                pe.wait_ge(row_live, 1)
                pe.wait_ge(w_out, 8)
                pe.matmul(bank[0:EP, 6, 0:1], before[0:EP, 0:EP], e_sm[0:EP, TOT:TOT + 1], start=True, stop=True)
                pe.matmul(bank[:, 6, 1:2], ones[0:EP, :], e_sm[0:EP, TOT:TOT + 1],
                          start=True, stop=True).then_inc(prefix_mm, 1)

            def edge_compact():
                pe.wait_ge(onehot_set, 1)
                for k in range(EC):
                    last = pe.matmul(bank[:, 7, 0:3], onehot[0:EP, k, :], pair_h[0:EP, k, :],
                                     start=(k == 0), stop=(k == EC - 1))
                last.then_inc(compact_mm, 1)

            def edge_broadcast():
                pe.wait_ge(bc_rhs, 1)
                pe.matmul(bank[:, 6, 0:P], ones[:], tmp[:], start=True, stop=True)
                pe.matmul(bank[:, 6, P:2 * P], ones[:], other_row[:], start=True, stop=True).then_inc(bc_mm, 1)

            def edge_x_transposes():
                pe.wait_ge(x_edges_in, 32)
                pe.wait_ge(w_out, 8)
                pe.wait_ge(bc_read, 1)
                for n, src in enumerate((xi, xj)):
                    for c in range(DC):
                        last = pe.transpose(bank[:, 6 + n, blk(c)], src[:, blk(c)], ident[:])
                last.then_inc(xt_tr, 1)

            def edge_project():
                pe.wait_ge(xt_out, 2)
                pe.wait_ge(b_in, 32)
                for n in range(2):
                    for c in range(DC):
                        pe.matmul(bank[:, 6 + n, :], xT[:, n, c, :], wt[:, n, c, :], start=(c == 0), stop=False)
                    last = pe.matmul(bank[:, 6 + n, :], ones[32 * n:32 * n + 1, :], bias[32 * n:32 * n + 1, :], start=False, stop=True)
                last.then_inc(qk_mm, 1)

            def edge_score_rows():
                pe.wait_ge(score_rhs, 1)
                for n in range(2):
                    last = pe.matmul(bank[:, 6 + n, :], ones[:],
                                     xT[:, n, :, :].rearrange("p c e -> p (c e)"), start=True, stop=True)
                last.then_inc(score_mm, 1)

            def edge_sums():
                pe.wait_ge(pw_set, 1)
                pe.matmul(bank[:, 6, 0:HEADS + 1], same_row[:], pw[:], start=True, stop=True).then_inc(z_mm, 1)

            def edge_table():
                pe.wait_ge(table_rhs, 1)
                for t in range(NT):
                    last = pe.matmul(bank[:, 7, 4 * t:4 * t + 3], edge_row[:, blk(t)], trow[:, 0:3],
                                     start=True, stop=True)
                last.then_inc(table_mm, 1)

            pe.wait_ge(consts, 1)
            pe.wait_ge(max_diag, 1)
            pe.matmul(bank[:, 6, 0:P], ones[:], same_row[:], start=True, stop=True).then_inc(max_mm, 1)
            transposes(0)
            transposes(1)
            for b in range(4):
                pe.wait_ge(hi_done, b + 1)
                pe.wait_ge(lo_done, b + 1)
                adj_x(0, 4 * b, 4 * b + 4)
                adj_x(1, 4 * b, 4 * b + 4)
            transposes(2)
            for I in range(1, NT):
                if I >= 2:
                    adj_x(I)
                if I + 2 < NT:
                    transposes(I + 2)
                if I in (2, 3, 6, 7):
                    w_transposes((2, 3, 6, 7).index(I))
                if I == 9:
                    edge_prefix()
                if I == 10:
                    edge_compact()
                if I == 11:
                    edge_broadcast()
                if I == 12:
                    edge_x_transposes()
                    edge_project()
                if I == 13:
                    edge_score_rows()
                if I == 14:
                    edge_sums()
            edge_table()

            def general_products(pe):
                def w_transposed(n):
                    pe.wait_ge(gen_w_in, 16 * n)
                    for c in range(DC):
                        for o in range(DC):
                            last = pe.transpose(bank[:, c, blk(o)], gw_raw[:, o, blk(c)], ident[:])
                    last.then_inc(gen_w_tr, 1)
                    pe.wait_ge(gen_w_out, n)

                def project(n, bias_row):
                    pe.wait_ge(gen_x_in, n * 16)
                    for c in range(DC):
                        last = pe.transpose(bank[:, 0, blk(c)], gx[:, blk(c)], ident[:])
                    last.then_inc(gen_x_tr, 1)
                    pe.wait_ge(gen_x_out, n)
                    for o in range(DC):
                        for c in range(DC):
                            pe.matmul(bank[:, 1, blk(o)], gwT[:, c, blk(o)], gxT[:, c, :], start=(c == 0), stop=False)
                        last = pe.matmul(bank[:, 1, blk(o)], bias[bias_row:bias_row + 1, blk(o)],
                                         ones[bias_row:bias_row + 1, :], start=False, stop=True)
                    last.then_inc(gen_p_mm, 1)

                def pair_product(n, start, stop):
                    pe.wait_ge(gen_hot, n)
                    for c in range(4):
                        last = pe.matmul(bank[:, 2 + c, :], row_hot[0:EP, :], col_hot[0:EP, c * 512:(c + 1) * 512],
                                         start=start, stop=stop)
                    last.then_inc(gen_pair_mm, 1)

                pe.wait_ge(gen_start, 1)
                pe.wait_ge(g_out, NT)
                w_transposed(1)
                with pe.Fori(0, NT) as J:
                    pe.wait_ge(gen_k_out, J + 1)
                    project(J + 1, 32)
                pe.wait_ge(gen_k_out, NT + 1)
                w_transposed(2)
                pe.sem_inc(gen_v_mm, 1)
                with pe.Fori(0, NT) as I:
                    pe.wait_ge(gen_row, I + 1)
                    project(I + (NT + 1), 0)
                    pair_product(I * EC + 1, True, False)
                    with pe.Fori(1, EC - 1) as k:
                        pair_product(I * EC + k + 1, False, False)
                    pair_product(I * EC + EC, False, True)
                    pe.wait_ge(gen_q_out, I + 1)
                    pe.wait_ge(gen_masks, I + 1)
                    for h in range(HEADS):
                        if h:
                            pe.wait_ge(gen_s_read, I * HEADS + h)
                        half = slice(DK * (h % 2), DK * (h % 2) + DK)
                        for c in range(4):
                            last = pe.matmul(bank[:, 2 + c, :], qT[half, h // 2, :],
                                             kT[half, h // 2, c * 512:(c + 1) * 512], start=True, stop=True)
                        last.then_inc(gen_s_mm, 1)
                    pe.wait_ge(gen_factor, I + 1)
                    for J in range(NT):
                        last = pe.transpose(bank[:, 2 + J // 4, blk(J % 4)], factor[:, blk(J)], ident[:])
                    last.then_inc(gen_f_tr, 1)
                    pe.wait_ge(gen_f_out, I + 1)
                    for q in range(4):
                        pe.wait_ge(gen_v_in, I * 64 + 16 * (q + 1))
                        for r in range(4):
                            J = 4 * q + r
                            last = pe.matmul(bank[:, 6, :], fT[:, blk(J)], v_stage[:, r, :],
                                             start=(J == 0), stop=(J == NT - 1))
                        last.then_inc(gen_v_mm, 1)
                pe.wait_ge(gen_done, 1)

            with pe.If(pe.value_load(n_live[0:1, 0:1]) > P):
                general_products(pe)

            def correct(t):
                if t == 2:
                    pe.wait_ge(coef_set, 1)
                if t >= 3:
                    pe.wait_ge(x1_pre, t - 2)
                pe.matmul(bank[:, (0, 1, 7)[t % 3], :], edge_row[:, blk(t)], xi[:],
                          start=True, stop=True).then_inc(corr_mm, 1)

            for t in range(3):
                correct(t)
            pe.wait_ge(g_out, NT)
            for J in range(NT):
                if J + 3 < NT:
                    correct(J + 3)
                pe.wait_ge(uh_done, J + 1)
                pe.wait_ge(ul_done, J + 1)
                for m in range(KOUT):
                    for k, u in enumerate((u_hi, u_lo)):
                        last = pe.matmul(bank[:, bank_of(m), :], sym[:, J, blk(m)], u(J),
                                         start=(J == 0 and k == 0), stop=(J == NT - 1 and k == 1))
                    if J == NT - 1:
                        last.then_inc(z1_mm, 1)

            def free_bank(n, eng):
                if n < 8:
                    eng.wait_ge(x1_pre, NT)
                elif n < NT + 8:
                    eng.wait_ge(vl_done, n - 7)
                else:
                    eng.wait_ge(y_read, n - NT - 7)

            for n in range(KOUT, NT):
                free_bank(n, pe)
                for J in range(NT):
                    for k, u in enumerate((u_hi, u_lo)):
                        last = pe.matmul(bank[:, bank_of(n), :], sym[:, J, blk(n)], u(J),
                                         start=(J == 0 and k == 0), stop=(J == NT - 1 and k == 1))
                last.then_inc(z1_mm, 1)

            def adj_v(I, J0, J1):
                for J in range(J0, J1):
                    pe.wait_ge(vh_done, J + 1)
                    pe.wait_ge(vl_done, J + 1)
                    for k, v in enumerate((v_hi, v_lo)):
                        last = pe.matmul(bank[:, bank_of(NT + I), :], at[:, J, blk(I)], v(J),
                                         start=(J == 0 and k == 0), stop=(J == NT - 1 and k == 1))
                return last

            free_bank(NT, pe)
            adj_v(0, 0, NT - 1)
            free_bank(NT + 1, pe)
            adj_v(1, 0, NT - 1)
            adj_v(0, NT - 1, NT).then_inc(y_mm, 1)
            adj_v(1, NT - 1, NT).then_inc(y_mm, 1)
            for I in range(2, NT):
                free_bank(NT + I, pe)
                adj_v(I, 0, NT).then_inc(y_mm, 1)

        @block.scalar
        def _(act):
            def cast_rows(I):
                act.wait_ge(a_in[I % 2], 16 * (I // 2 + 1))
                if I >= 2:
                    act.wait_ge(tr_done, I - 1)
                    act.wait_ge(arow_read, I - 1)
                act.activation(arow[:, I % 2, :], stage[:, I % 2, :], ACT.Copy,
                               accum_out=row_sum[:, I:I + 1]).then_inc(cast_done, 1)

            def save_at(I):
                act.wait_ge(tr_done, I + 1)
                act.copy(at[:, :, blk(I)], tp(I).rearrange("p (j i) -> p j i", i=P),
                         saturate=False).then_inc(at_act, 1)

            def split_x(b):
                cols = slice(4 * b * D, (4 * b + 4) * D)
                src = g[:, 4 * b:4 * b + 4, :].rearrange("p t d -> p (t d)")
                act.wait_ge(x_in[b], 16)
                act.wait_ge(scale_set, 1)
                act.activation(xs16[:, 0, cols], src, ACT.Copy, scale=xscale[:, 5:6]).then_inc(hi_done, 1)

            cast_rows(0)
            split_x(0)
            split_x(1)
            save_at(0)
            cast_rows(1)
            split_x(2)
            save_at(1)
            split_x(3)
            cast_rows(2)
            for I in range(NT):
                if I + 2 < NT:
                    save_at(I + 2)
                if I + 3 < NT:
                    cast_rows(I + 3)
                act.wait_ge(g_mm, I + 1)
                if I == 0:
                    act.wait_ge(lo_done, 4)
                act.copy(g[:, I, :], bank[:, 4 + I % 2, :]).then_inc(g_out, 1)
                if I in (2, 3, 6, 7):
                    n = (2, 3, 6, 7).index(I)
                    for c in range(2):
                        act.wait_ge(w_tr, 2 * n + c + 1)
                        act.copy(wt[:, n // 2, 2 * (n % 2) + c, :], bank[:, 6 + c, :]).then_inc(w_out, 1)
                if I == 12:
                    act.wait_ge(xt_tr, 1)
                    for n in range(2):
                        act.copy(xT[:, n, :, :].rearrange("p c e -> p (c e)"), bank[:, 6 + n, :]).then_inc(xt_out, 1)
                if I == 13:
                    act.wait_ge(args_set, 1)
                    act.activation(exps[:], args[:], ACT.Exp).then_inc(exp_done, 1)
            act.wait_ge(deg_set, 1)
            act.sqrt(rt[:, T3, :], deg[:]).then_inc(deg_root, 1)
            with act.If(act.value_load(n_live[0:1, 0:1]) > P):
                with act.Fori(0, NT) as I:
                    for h in range(HEADS):
                        act.wait_ge(gen_max, I * HEADS + (h + 1))
                        act.activation(d_score, d_score, ACT.Exp, bias=mv[:, 0, 1:2],
                                       accum_out=mv[:, 0, 2:3]).then_inc(gen_exp, 1)
            for t in range(NT + 1):
                if t < NT:
                    act.wait_ge(var1_set, t + 1)
                    act.sqrt(mv[:, t % 4, 3:4], mv[:, t % 4, 2:3]).then_inc(root1, 1)
                if t:
                    m = mv[:, (t - 1) % 4, :]
                    act.wait_ge(norm1_set, t)
                    act.activation(g[:, t - 1, :], g[:, t - 1, :], ACT.Identity, bias=m[:, 5:6],
                                   scale=m[:, 4:5]).then_inc(x1_done, 1)
                    act.wait_ge(x1_done, t)
                    if t == 1:
                        act.wait_ge(g_mm, NT)
                    act.activation(u_hi(t - 1), g[:, t - 1, :], ACT.Copy,
                                   scale=rt[:, SDINV, t - 1:t]).then_inc(uh_done, 1)
            for t in range(NT):
                act.wait_ge(z1_mm, t + 1)
                act.activation(v_hi(t), bank[:, bank_of(t), :], ACT.Copy,
                               scale=rt[:, SCALE_V, t:t + 1]).then_inc(vh_done, 1)
            for t in range(NT + 1):
                if t < NT:
                    act.wait_ge(var2_set, t + 1)
                    act.sqrt(mv[:, t % 4, 3:4], mv[:, t % 4, 2:3]).then_inc(root2, 1)
                if t:
                    act.wait_ge(fin_pre, t)
                    act.activation(g[:, t - 1, :], g[:, t - 1, :], ACT.Identity, bias=mv[:, (t - 1) % 4, 5:6],
                                   scale=mv[:, (t - 1) % 4, 4:5]).then_inc(fin, 1)

        @block.vector
        def _(dve):
            links = [0]

            def link(ins):
                links[0] += 1
                ins.then_inc(chain, 1)
                dve.wait_ge(chain, links[0])

            def mark(ins):
                links[0] += 1
                ins.then_inc(chain, 1)
                return links[0]

            mark(dve.memset(ones[:], 1.0))
            mark(dve.memset(col_part[:], 0.0))
            mark(dve.memset(pair_h[:], 1.0))
            dve.wait_ge(iota_set, 2)
            link(dve.tensor_copy(iota[:], iota_i))
            link(dve.tensor_scalar(identb[:], iota[:, 0:P], iota[:, P:P + 1], None, ALU.is_equal))
            mark(dve.tensor_scalar(ident[:], iota[:, 0:P], iota[:, P:P + 1], None, ALU.is_equal))
            mark(dve.tensor_scalar(ident2[:], identb[:], 2.0, None, ALU.mult))
            dve.tensor_scalar(before[:], iota[:, 0:P], iota[:, P:P + 1], None, ALU.is_gt).then_inc(consts, 1)
            dve.wait_ge(pairs_in, 16)
            link(dve.tensor_copy(pair_f[0:EP], pair_i[0:EP]))
            dve.scalar_tensor_tensor(flat[0:EP], pair_f[0:EP, :, 0], float(N), pair_f[0:EP, :, 1],
                                     ALU.mult, ALU.add).then_inc(flat_ready, 1)
            dve.tensor_copy(pair_h[0:EP, :, 0:2], pair_f[0:EP]).then_inc(flat_ready, 1)

            def column_sums(I):
                dve.tensor_reduce(col_part[:, :, I], tp(I).rearrange("p (j i) -> p j i", i=P),
                                  AX, ALU.add).then_inc(cols_summed, 1)

            def symmetrise(I):
                w = (I + 1) * P
                dve.wait_ge(cast_done, I + 1)
                dve.wait_ge(at_act, I + 1)
                column_sums(I)
                dve.scalar_tensor_tensor(tmp_junk, arow[:, I % 2, blk(I)], 1.0, identb[:], ALU.mult, ALU.mult,
                                         accum_out=diag[:, I:I + 1])
                if I + 1 < NT:
                    mark(dve.tensor_copy(sym[:, I, w:N], arow[:, I % 2, w:N], saturate=False))
                link(dve.scalar_tensor_tensor(sym[:, I, 0:w], arow[:, I % 2, 0:w], 1.0, at[:, I, 0:w],
                                              ALU.mult, ALU.add, saturate=False))
                mark(dve.tensor_tensor(sym[:, I, blk(I)], sym[:, I, blk(I)], ident2[:], ALU.add, saturate=False)
                     ) if I else link(dve.tensor_tensor(sym[:, I, blk(I)], sym[:, I, blk(I)], ident2[:], ALU.add, saturate=False))
                if I:
                    link(dve.tensor_tensor(sym[:, 0:I, blk(I)], sym[:, 0:I, blk(I)], at[:, 0:I, blk(I)], ALU.add, saturate=False))
                dve.tensor_copy(mv[:, 0, 0:1], diag[:, I:I + 1]).then_inc(arow_read, 1)

            tmp_junk = junk[:]

            for b in range(4):
                dve.wait_ge(x_in[b], 16)
                last = mark(dve.tensor_reduce(xscale[:, b:b + 1],
                                              g[:, 4 * b:4 * b + 4, :].rearrange("p t d -> p (t d)"),
                                              AX, ALU.max, apply_absolute_value=True))
            dve.wait_ge(chain, last)
            link(dve.tensor_reduce(xscale[:, 4:5], xscale[:, 0:4], AX, ALU.max))
            dve.tensor_scalar(same_row[:], ident[:], xscale[:, 4:5], None, ALU.mult).then_inc(max_diag, 1)
            dve.wait_ge(max_mm, 1)
            link(dve.tensor_reduce(xscale[:, 4:5], bank[:, 6, 0:P], AX, ALU.max))
            link(dve.tensor_scalar(xscale_i[:, 4:5], xscale_i[:, 4:5], 0x7F800000, None, ALU.bitwise_and))
            link(dve.tensor_scalar(xscale_i[:, 5:6], xscale_i[:, 4:5], -1.0, float((254 + 10) << 23),
                                   ALU.mult, ALU.add))
            dve.tensor_scalar(xscale_i[:, 6:7], xscale_i[:, 5:6], -1.0, float(254 << 23),
                              ALU.mult, ALU.add).then_inc(scale_set, 1)

            def split_x(b):
                cols = slice(4 * b * D, (4 * b + 4) * D)
                src = g[:, 4 * b:4 * b + 4, :].rearrange("p t d -> p (t d)")
                dve.wait_ge(hi_done, b + 1)
                dve.scalar_tensor_tensor(xs16[:, 1, cols], src, xscale[:, 5:6], xs16[:, 0, cols],
                                         ALU.mult, ALU.subtract).then_inc(lo_done, 1)

            for b in range(4):
                split_x(b)
            symmetrise(0)
            symmetrise(1)

            def edge_live():
                dve.wait_ge(adj_e_in, 16 * EC)
                link(dve.tensor_tensor(order[0:EP], pair_f[0:EP, :, 0], pair_f[0:EP, :, 1], ALU.not_equal))
                link(dve.scalar_tensor_tensor(live[0:EP], adj_e[0:EP], 1.0, order[0:EP], ALU.is_equal, ALU.mult))
                dve.tensor_reduce(e_sm[0:EP, TOT:TOT + 1], live[0:EP], AX, ALU.add).then_inc(row_live, 1)

            def edge_onehot():
                dve.wait_ge(prefix_mm, 1)
                mark(dve.tensor_copy(n_live[:], bank[:, 6, 1:2]))
                link(dve.tensor_copy(e_sm[0:EP, W1:W1 + 1], bank[0:EP, 6, 0:1]))
                link(dve.tensor_tensor_scan(order[0:EP], ones[0:EP, 0:EC], live[0:EP], e_sm[0:EP, W1:W1 + 1],
                                            ALU.mult, ALU.add))
                link(dve.tensor_tensor(order[0:EP], order[0:EP], live[0:EP], ALU.mult))
                dve.tensor_tensor(onehot[0:EP], order[0:EP].rearrange("p (k o) -> p k o", o=1).broadcast_to((EP, EC, P)),
                                  iota[0:EP, 0:P].rearrange("p (o m) -> p o m", o=1).broadcast_to((EP, EC, P)),
                                  ALU.is_equal, saturate=False).then_inc(onehot_set, 1)

            def edge_list():
                dve.wait_ge(compact_mm, 1)
                link(dve.tensor_copy(e_sm[:, 0:3], bank[:, 7, 0:3]))
                dve.tensor_copy(e_idx[:], e_sm[:, 0:2]).then_inc(edge_idx, 1)
                link(dve.scalar_tensor_tensor(ec(IV), ec(I_), -1.0, ec(V_), ALU.add, ALU.add))
                mark(dve.tensor_scalar(ec(EMPTY), ec(V_), -1.0, 1.0, ALU.mult, ALU.add))
                link(dve.scalar_tensor_tensor(ec(FV), ec(I_), float(N), ec(J_), ALU.mult, ALU.add))
                link(dve.scalar_tensor_tensor(ec(FV), ec(FV), -1.0, ec(V_), ALU.add, ALU.add))
                mark(dve.tensor_scalar(tmp[:], ident[:], ec(IV), None, ALU.mult))
                dve.tensor_scalar(other_row[:], ident[:], ec(FV), None, ALU.mult).then_inc(bc_rhs, 1)

            def edge_masks():
                dve.wait_ge(bc_mm, 1)
                link(dve.tensor_scalar(same_row[:], bank[:, 6, P:2 * P], ec(FV), 0.0, ALU.is_equal, ALU.add,
                                       accum_out=ec(MULT)))
                link(dve.tensor_scalar(same_row[:], bank[:, 6, 0:P], ec(IV), 0.0, ALU.is_equal, ALU.add,
                                       accum_out=ec(SAME)))
                dve.tensor_scalar(other_row[:], same_row[:], -1.0, BIG, ALU.add, ALU.mult).then_inc(bc_read, 1)
                link(dve.reciprocal(e_sm[:, MULT:SAME + 1], e_sm[:, MULT:SAME + 1]))
                link(dve.tensor_scalar(e_sm[:, MULT:SAME + 1], e_sm[:, MULT:SAME + 1], ec(V_), None, ALU.mult))


            def edge_scores():
                dve.wait_ge(qk_mm, 1)
                link(dve.tensor_copy(xi[:], bank[:, 6, :]))
                link(dve.tensor_tensor(xi[:], xi[:], bank[:, 7, :], ALU.mult))
                link(dve.tensor_reduce(score[:], xi[:].rearrange("p (h d) -> p h d", h=HEADS), AX, ALU.add))
                link(dve.tensor_scalar(score[:], score[:], float(DK) ** -0.5, None, ALU.mult))
                dve.tensor_tensor(masked, score[:].rearrange("p (h o) -> p h o", o=1).broadcast_to((P, HEADS, P)),
                                  ident[:].rearrange("p (o m) -> p o m", o=1).broadcast_to((P, HEADS, P)),
                                  ALU.mult).then_inc(score_rhs, 1)
                link(dve.tensor_scalar(rt[:, T1, :], iota[:, 0:NT], -float(P), ec(I_), ALU.mult, ALU.add))
                link(dve.tensor_scalar(rt[:, T1, :], rt[:, T1, :], float(P) + 1.0, None, ALU.add))
                link(dve.tensor_tensor(edge_row.rearrange("p (t m) -> p t m", m=P),
                                       rt[:, T1, :].rearrange("p (t o) -> p t o", o=1).broadcast_to((P, NT, P)),
                                       iota[:, 0:P].rearrange("p (o m) -> p o m", o=1).broadcast_to((P, NT, P)),
                                       ALU.is_equal))
                dve.wait_ge(rows_in, 16)
                link(dve.tensor_reduce(ec(ROWC), adj_rows, AX, ALU.add))
                link(dve.tensor_tensor(adj_rows, adj_rows, edge_row, ALU.mult))
                link(dve.tensor_reduce(ec(DG), adj_rows, AX, ALU.add))
                link(dve.tensor_tensor(ec(CNT), ec(ROWC), ec(DG), ALU.subtract))

            def edge_max():
                dve.wait_ge(score_mm, 1)
                link(dve.tensor_tensor(masked, bank[:, 6:8, :].rearrange("p a (c e) -> p (a c) e", e=P),
                                       other_row[:].rearrange("p (o m) -> p o m", o=1).broadcast_to((P, HEADS, P)),
                                       ALU.add))
                link(dve.tensor_reduce(zz[:, 0, :], masked, AX, ALU.max))
                link(dve.tensor_scalar(args[:, 0, :], zz[:, 0, :], SELF_SCORE, -1.0, ALU.max, ALU.mult))
                mark(dve.tensor_scalar(args[:, 1, :], args[:, 0, :], SELF_SCORE, None, ALU.add))
                dve.tensor_tensor(args[:, 2, :], args[:, 0, :], score[:], ALU.add).then_inc(args_set, 1)
                dve.wait_ge(exp_done, 1)
                mark(dve.tensor_scalar(pw[:, 0:HEADS], exps[:, 2, :], ec(MULT), None, ALU.mult))
                dve.tensor_copy(pw[:, HEADS:HEADS + 1], ec(MULT)).then_inc(pw_set, 1)

            def edge_weights():
                dve.wait_ge(z_mm, 1)
                link(dve.tensor_tensor(ec(CNT), ec(CNT), bank[:, 6, HEADS:HEADS + 1], ALU.subtract))
                link(dve.scalar_tensor_tensor(zz[:, 1, :], exps[:, 0, :], ec(CNT), exps[:, 1, :], ALU.mult, ALU.add))
                link(dve.tensor_tensor(zz[:, 1, :], zz[:, 1, :], bank[:, 6, 0:HEADS], ALU.add))
                link(dve.tensor_scalar(zz[:, 1, :], zz[:, 1, :], ec(EMPTY), float(HEADS), ALU.add, ALU.mult))
                link(dve.reciprocal(zz[:, 1, :], zz[:, 1, :]))
                for n, w in enumerate((W1, W2, W3)):
                    link(dve.tensor_tensor(zz[:, 2, :], exps[:, n, :], zz[:, 1, :], ALU.mult))
                    link(dve.tensor_reduce(ec(w), zz[:, 2, :], AX, ALU.add))
                link(dve.tensor_tensor(ec(W3), ec(W3), ec(W1), ALU.subtract))
                link(dve.tensor_tensor(ec(W3), ec(W3), ec(MULT), ALU.mult))
                mark(dve.tensor_scalar(xi[:], xj[:], ec(W3), None, ALU.mult))
                mark(dve.tensor_copy(trow[:, 0:1], ec(SAME)))
                dve.tensor_scalar(trow[:, 1:3], e_sm[:, W1:W2 + 1], ec(SAME), None, ALU.mult).then_inc(table_rhs, 1)

            def inverse_root(v, root, out, w):
                link(dve.reciprocal(out, root))
                link(dve.tensor_tensor(w, out, out, ALU.mult))
                link(dve.tensor_tensor(w, w, v, ALU.mult))
                link(dve.tensor_scalar(w, w, -0.5, 1.5, ALU.mult, ALU.add))
                link(dve.tensor_tensor(out, out, w, ALU.mult))

            def row_degrees():
                em0 = float(np_exp(-SELF_SCORE))
                r = lambda k: rt[:, k, :]
                link(dve.tensor_tensor(r(T1), row_sum[:], diag[:], ALU.subtract))
                link(dve.tensor_scalar(r(T1), r(T1), em0, 1.0, ALU.mult, ALU.add))
                link(dve.reciprocal(r(T1), r(T1)))
                link(dve.tensor_reduce(r(T2), col_part[:], AX, ALU.add))
                link(dve.tensor_tensor(r(T2), r(T2), row_sum[:], ALU.add))
                link(dve.tensor_scalar(r(T2), r(T2), 0.5, 1.0, ALU.mult, ALU.add))
                dve.tensor_copy(deg[:], r(T2)).then_inc(deg_set, 1)
                dve.wait_ge(deg_root, 1)
                inverse_root(deg[:], r(T3), r(T2), r(SDINV))
                mark(dve.tensor_scalar(r(SDINV), r(T2), U_SCALE, None, ALU.mult))
                link(dve.tensor_scalar(r(SCALE_V), r(T2), 0.5 * V_SCALE / U_SCALE, None, ALU.mult))

            def row_coefficients():
                tab = bank[:, 7, 0:4 * NT].rearrange("p (t c) -> p c t", c=4)
                em0 = float(np_exp(-SELF_SCORE))
                r = lambda k: rt[:, k, :]
                dve.wait_ge(table_mm, 1)
                link(dve.tensor_scalar(r(T3), tab[:, 0, :], -1.0, 1.0, ALU.mult, ALU.add))
                link(dve.tensor_tensor(r(T3), r(T3), r(T1), ALU.mult))
                mark(dve.scalar_tensor_tensor(r(ALPHA), r(T3), em0, tab[:, 1, :], ALU.mult, ALU.add))
                ins = dve.tensor_tensor(r(BETA), r(T3), tab[:, 2, :], ALU.add)
                ins.then_inc(coef_set, 1)
                dve.wait_ge(coef_set, 1)
                link(dve.tensor_tensor(r(T3), r(ALPHA), diag[:], ALU.mult))
                mark(dve.tensor_scalar(r(ALPHA), r(ALPHA), xscale[:, 6:7], None, ALU.mult))
                link(dve.scalar_tensor_tensor(r(BETA), r(BETA), 1.0, r(T3), ALU.add, ALU.subtract))

            for I in range(NT):
                if I + 2 < NT:
                    symmetrise(I + 2)
                if I == 8:
                    edge_live()
                if I == 9:
                    edge_onehot()
                if I == 10:
                    edge_list()
                if I == 11:
                    edge_masks()
                if I == 12:
                    edge_scores()
                if I == 13:
                    edge_max()
                if I == 14:
                    edge_weights()
                    row_degrees()
            row_coefficients()

            def general_path(dve):
                shift, tile_no = mv[:, 1, 0:1], mv[:, 1, 1:2]
                n_sem = [0]

                def step(ins):
                    ins.then_inc(gen_step, 1)
                    dve.wait_ge(gen_step, 1)
                    dve.sem_clear(gen_step)

                def w_out(n):
                    dve.wait_ge(gen_w_tr, n)
                    dve.tensor_copy(gwT.rearrange("p c d -> p (c d)"),
                                    bank[:, 0:4, :].rearrange("p a b -> p (a b)")).then_inc(gen_w_out, 1)

                def x_out(n):
                    dve.wait_ge(gen_x_tr, n)
                    dve.tensor_copy(xi[:], bank[:, 0, :]).then_inc(gen_x_out, 1)
                    dve.wait_ge(gen_p_mm, n)

                def hot(k, n):
                    step(dve.tensor_scalar(rt[0:EP, T1, :], iota[0:EP, 0:NT], -float(P), float(P) + 1.0,
                                           ALU.mult, ALU.add))
                    step(dve.tensor_scalar(rt[0:EP, T1, :], rt[0:EP, T1, :], pair_f[0:EP, bass.ds(k, 1), 1], None, ALU.add))
                    mark_g(dve.tensor_scalar(row_hot[0:EP, :], iota[0:EP, 0:P], shift[0:EP],
                                             pair_f[0:EP, bass.ds(k, 1), 0], ALU.add, ALU.is_equal))
                    dve.tensor_tensor(col_hot[0:EP, :].rearrange("p (t m) -> p t m", m=P),
                                      rt[0:EP, T1, :].rearrange("p (t o) -> p t o", o=1).broadcast_to((EP, NT, P)),
                                      iota[0:EP, 0:P].rearrange("p (o m) -> p o m", o=1).broadcast_to((EP, NT, P)),
                                      ALU.is_equal).then_inc(gen_hot, 1)

                def mark_g(ins):
                    pass

                dve.wait_ge(g_mm, NT)
                dve.wait_ge(g_out, NT)
                dve.memset(shift, -1.0)
                step(dve.memset(tile_no, 1.0))
                dve.sem_inc(gen_start, 1)
                w_out(1)
                dve.sem_inc(gen_k_out, 1)
                with dve.Fori(0, NT) as J:
                    x_out(J + 1)
                    dve.tensor_copy(kT[:, :, bass.ds(J * P, P)],
                                    bank[:, 1, :].rearrange("p (c e) -> p c e", c=DC)).then_inc(gen_k_out, 1)
                w_out(2)
                dve.sem_inc(gen_row, 1)
                with dve.Fori(0, NT) as I:
                    x_out(I + (NT + 1))
                    dve.tensor_copy(qT, bank[:, 1, :].rearrange("p (c e) -> p c e", c=DC)).then_inc(gen_q_out, 1)
                    hot(0, I)
                    with dve.Fori(1, EC) as k:
                        dve.wait_ge(gen_pair_mm, I * EC + k)
                        hot(k, I)
                    dve.wait_ge(gen_pair_mm, I * EC + EC)
                    step(dve.tensor_scalar(rt[:, T1, :], iota[:, 0:NT], tile_no, iota[:, P:P + 1],
                                           ALU.is_equal, ALU.mult))
                    step(dve.tensor_tensor(factor.rearrange("p (t m) -> p t m", m=P),
                                           rt[:, T1, :].rearrange("p (t o) -> p t o", o=1).broadcast_to((P, NT, P)),
                                           iota[:, 0:P].rearrange("p (o m) -> p o m", o=1).broadcast_to((P, NT, P)),
                                           ALU.is_equal))
                    step(dve.tensor_scalar(d_score, factor, -1.0, 1.0, ALU.mult, ALU.add))
                    dve.wait_ge(gen_a_in, I * 16 + 16)
                    step(dve.tensor_scalar(floor, fT, 1.0, -1.0, ALU.is_equal, ALU.add))
                    step(dve.scalar_tensor_tensor(floor, floor, BIG, d_score, ALU.mult, ALU.mult))
                    step(dve.scalar_tensor_tensor(floor, factor, SELF_SCORE, floor, ALU.mult, ALU.add))
                    dve.scalar_tensor_tensor(pair_mask, bank[:, 2:6, :].rearrange("p a b -> p (a b)"), 1.0, d_score,
                                             ALU.min, ALU.mult).then_inc(gen_masks, 1)
                    step(dve.memset(factor, 0.0))
                    for h in range(HEADS):
                        dve.wait_ge(gen_masks, I + 1)
                        dve.wait_ge(gen_s_mm, I * HEADS + (h + 1))
                        ins = dve.scalar_tensor_tensor(d_score, bank[:, 2:6, :].rearrange("p a b -> p (a b)"),
                                                       float(DK) ** -0.5, pair_mask, ALU.mult, ALU.mult)
                        ins.then_inc(gen_s_read, 1)
                        dve.wait_ge(gen_s_read, I * HEADS + (h + 1))
                        step(dve.tensor_tensor(d_score, d_score, floor, ALU.add))
                        step(dve.tensor_reduce(mv[:, 0, 0:1], d_score, AX, ALU.max))
                        dve.tensor_scalar(mv[:, 0, 1:2], mv[:, 0, 0:1], -1.0, None, ALU.mult).then_inc(gen_max, 1)
                        dve.wait_ge(gen_exp, I * HEADS + (h + 1))
                        step(dve.tensor_scalar(mv[:, 0, 3:4], mv[:, 0, 2:3], float(HEADS), None, ALU.mult))
                        step(dve.reciprocal(mv[:, 0, 3:4], mv[:, 0, 3:4]))
                        ins = dve.scalar_tensor_tensor(factor, d_score, mv[:, 0, 3:4], factor, ALU.mult, ALU.add)
                        if h < HEADS - 1:
                            step(ins)
                        else:
                            ins.then_inc(gen_factor, 1)
                    dve.wait_ge(gen_f_tr, I + 1)
                    dve.tensor_copy(fT, bank[:, 2:6, :].rearrange("p a b -> p (a b)")).then_inc(gen_f_out, 1)
                    dve.tensor_scalar(shift, shift, float(P), None, ALU.add)
                    step(dve.tensor_scalar(tile_no, tile_no, 1.0, None, ALU.add))
                    dve.wait_ge(gen_v_mm, I * 4 + 5)
                    dve.tensor_copy(g[:, bass.ds(I, 1), :], bank[:, 6:7, :]).then_inc(gen_row, 1)
                dve.memset(xi[:], 0.0)
                dve.memset(rt[:, ALPHA, :], 1.0)
                step(dve.memset(rt[:, BETA, :], 1.0))
                dve.wait_ge(gen_row, NT + 1)
                dve.sem_inc(gen_done, 1)

            with dve.If(dve.value_load(n_live[0:1, 0:1]) > P):
                general_path(dve)

            def moments(t, var_set):
                m = mv[:, t % 4, :]
                link(dve.bn_stats(stats[:, t % 2, :], g[:, t, :]))
                link(dve.bn_aggr(m[:, 0:2], stats[:, t % 2, :]))
                dve.tensor_scalar(m[:, 2:3], m[:, 1:2], LN_EPS, None, ALU.add).then_inc(var_set, 1)

            for t in range(NT + 2):
                now, prev = t < NT, 1 <= t <= NT
                m, mp = mv[:, t % 4, :], mv[:, (t - 1) % 4, :]
                if now:
                    dve.wait_ge(corr_mm, t + 1)
                    dve.wait_ge(g_out, t + 1)
                    y_at = mark(dve.scalar_tensor_tensor(g[:, t, :], g[:, t, :], rt[:, ALPHA, t:t + 1],
                                                         bank[:, (0, 1, 7)[t % 3], :], ALU.mult, ALU.add))
                if prev:
                    dve.wait_ge(root1, t)
                    s_at = mark(dve.reciprocal(mp[:, 4:5], mp[:, 3:4]))
                if now:
                    dve.wait_ge(xr_in[t % NXR], 16 * (t // NXR + 1))
                    dve.wait_ge(chain, y_at)
                    dve.scalar_tensor_tensor(g[:, t, :], x_again(t), rt[:, BETA, t:t + 1], g[:, t, :],
                                             ALU.mult, ALU.add).then_inc(x1_pre, 1)
                if prev:
                    dve.wait_ge(chain, s_at)
                    s_at = mark(dve.scalar_tensor_tensor(mp[:, 6:7], mp[:, 4:5], mp[:, 2:3], mp[:, 4:5],
                                                         ALU.mult, ALU.mult))
                if t >= 2:
                    dve.wait_ge(uh_done, t - 1)
                    dve.scalar_tensor_tensor(u_lo(t - 2), g[:, t - 2, :], rt[:, SDINV, t - 2:t - 1], u_hi(t - 2),
                                             ALU.mult, ALU.subtract).then_inc(ul_done, 1)
                if prev:
                    dve.wait_ge(chain, s_at)
                    s_at = mark(dve.tensor_scalar(mp[:, 6:7], mp[:, 6:7], -0.5, 1.5, ALU.mult, ALU.add))
                if now:
                    dve.wait_ge(x1_pre, t + 1)
                    st_at = mark(dve.bn_stats(stats[:, t % 2, :], g[:, t, :]))
                if prev:
                    dve.wait_ge(chain, s_at)
                    s_at = mark(dve.tensor_tensor(mp[:, 4:5], mp[:, 4:5], mp[:, 6:7], ALU.mult))
                    dve.wait_ge(chain, s_at)
                    dve.scalar_tensor_tensor(mp[:, 5:6], mp[:, 0:1], -1.0, mp[:, 4:5],
                                             ALU.mult, ALU.mult).then_inc(norm1_set, 1)
                if now:
                    dve.wait_ge(chain, st_at)
                    link(dve.bn_aggr(m[:, 0:2], stats[:, t % 2, :]))
                    dve.tensor_scalar(m[:, 2:3], m[:, 1:2], LN_EPS, None, ALU.add).then_inc(var1_set, 1)
            for t in range(NT):
                dve.wait_ge(vh_done, t + 1)
                dve.scalar_tensor_tensor(v_lo(t), bank[:, bank_of(t), :],
                                         rt[:, SCALE_V, t:t + 1], v_hi(t),
                                         ALU.mult, ALU.subtract).then_inc(vl_done, 1)
            for t in range(NT + 1):
                if t < NT:
                    dve.wait_ge(y_mm, t + 1)
                    dve.scalar_tensor_tensor(g[:, t, :], bank[:, bank_of(NT + t), :], 1.0 / V_SCALE, g[:, t, :],
                                             ALU.mult, ALU.add).then_inc(y_read, 1)
                    dve.wait_ge(y_read, t + 1)
                    if t >= 4:
                        dve.wait_ge(fin, t - 3)
                    moments(t, var2_set)
                if t:
                    m = mv[:, (t - 1) % 4, :]
                    dve.wait_ge(root2, t)
                    inverse_root(m[:, 2:3], m[:, 3:4], m[:, 4:5], m[:, 6:7])
                    dve.scalar_tensor_tensor(m[:, 5:6], m[:, 0:1], -1.0, m[:, 4:5],
                                             ALU.mult, ALU.mult).then_inc(fin_pre, 1)


def np_exp(v):
    import numpy as np
    return np.exp(np.float64(v))


_INS = ['x', 'adj', 'L0_gnn_rel_pair_index', 'L0_gnn_Wq', 'L0_gnn_bq', 'L0_gnn_Wk', 'L0_gnn_bk']


def kernel(**inputs):
    import numpy as _np
    import concourse.bacc as _bacc
    from concourse import mybir as _mybir
    from concourse.bass_utils import run_bass_kernel_spmd as _run

    nc = _bacc.Bacc("TRN2", target_bir_lowering=False, num_devices=1)
    arrays, args = {}, []
    for name in _INS:
        a = _np.ascontiguousarray(inputs[name])
        arrays[f"in_{name}_dram"] = a
        args.append(nc.dram_tensor(f"in_{name}_dram", a.shape, _mybir.dt.from_np(a.dtype), kind="ExternalInput").ap())
    args.append(nc.dram_tensor("out_dram", args[0].shape, _mybir.dt.float32, kind="ExternalOutput").ap())
    gnn_residual_kernel(nc, *args)
    r = _run(nc, [arrays], core_ids=[0])
    return r.results[0]["out_dram"]
```

```python
from contextlib import ExitStack

import concourse.bass as bass
from concourse import mybir

P = 128
F32 = mybir.dt.float32
BF16 = mybir.dt.bfloat16
F16 = mybir.dt.float16
F8 = mybir.dt.float8e4
I32 = mybir.dt.int32
U32 = mybir.dt.uint32
ALU = mybir.AluOpType
ACT = mybir.ActivationFunctionType
AX = mybir.AxisListType.X

HEADS = 8
SELF_SCORE = 1e-07
LN_EPS = 1e-05
BIG = 3.0e38
U_SCALE = 64.0
V_SCALE = 32.0


def gnn_residual_kernel(nc, x, adj, pairs, wq, bq, wk, bk, out):
    N, D = x.shape
    E = pairs.shape[0]
    NT = N // P
    DC = D // P
    DK = D // HEADS
    EP = 125
    EC = E // EP
    assert EP * EC == E and NT == 16 and DC == 4
    KOUT = 5

    adj_flat = adj.rearrange("a b -> (a b)").rearrange("(n o) -> n o", o=1)
    x_tiles = x.rearrange("(t p) d -> p t d", p=P)
    out_tiles = out.rearrange("(t p) d -> p t d", p=P)

    with ExitStack() as ctx:
        def sb(name, shape, dt):
            return ctx.enter_context(nc.sbuf_tensor(name, shape, dt))

        def sem(name):
            return ctx.enter_context(nc.semaphore(name))

        bank = ctx.enter_context(nc.psum_tensor("bank", [P, 8, 512], F32))
        at = sb("at", [P, NT, N], F8)
        sym = sb("sym", [P, NT, N], F8)
        xs = sb("xs", [P, 3, NT * D], BF16)
        g = sb("g", [P, NT, D], F32)
        stage = sb("stage", [P, 2, N], F32)
        arow = sb("arow", [P, 2, N], BF16)
        scratch = sb("scratch", [P, 2048], F32)
        wt = sb("wt", [P, 2, DC, D], F32)
        xi = sb("xi", [P, D], F32)
        xj = sb("xj", [P, D], F32)
        bias = sb("bias", [33, D], F32)
        ones = sb("ones", [P, P], F32)
        iota = sb("iota", [P, P + 1], F32)
        ident = sb("ident", [P, P], F32)
        identb = sb("identb", [P, P], BF16)
        ident2 = sb("ident2", [P, P], BF16)
        pair_f = sb("pair_f", [P, EC, 2], F32)
        pair_h = sb("pair_h", [P, EC, 3], F16)
        flat = sb("flat", [P, EC], I32)
        adj_e = sb("adj_e", [P, EC], F32)
        live = sb("live", [P, EC], F32)
        order = sb("order", [P, EC], F32)
        e_sm = sb("e_sm", [P, 48], F32)
        e_idx = sb("e_idx", [P, 2], I32)
        n_live = sb("n_live", [P, 1], I32)
        same_row = sb("same_row", [P, P], F32)
        tmp = sb("tmp", [P, P], F32)
        junk = sb("junk", [P, P], BF16)
        other_row = sb("other_row", [P, P], F32)
        before = other_row
        iota_i = xi[:, 0:P + 1].bitcast(I32)
        pair_i = xj[:, 0:2 * EC].bitcast(I32).rearrange("p (k c) -> p k c", c=2)
        score = sb("score", [P, HEADS], F32)
        args = sb("args", [P, 3, HEADS], F32)
        exps = sb("exps", [P, 3, HEADS], F32)
        pw = sb("pw", [P, HEADS + 1], F32)
        zz = sb("zz", [P, 4, HEADS], F32)
        trow = sb("trow", [P, 4], F32)
        trow_b = sb("trow_b", [P, 3, 4], BF16)
        row_sum = sb("row_sum", [P, NT], F32)
        diag = sb("diag", [P, NT], F32)
        deg = sb("deg", [P, NT], F32)
        col_part = sb("col_part", [P, NT, NT], F32)
        rt = sb("rt", [P, 8, NT], F32)
        xscale = sb("xscale", [P, 16], F32)
        xscale_i = xscale[:].bitcast(I32)
        stats = sb("stats", [P, 2, 6], F32)
        mv = sb("mv", [P, 4, 8], F32)
        eps = sb("eps", [P, 1], F32)
        junk_root = sb("junk_root", [P, 1], F32)

        I_, J_, V_, IV, FV, EMPTY, CNT, MULT, SAME, W1, W2, W3, TOT = range(13)
        ec = lambda k: e_sm[:, k:k + 1]
        ALPHA, BETA, SDINV, SCALE_V, T1, T2, T3 = range(7)

        xs16 = xs[:].bitcast(F16)
        xpart = lambda k, t: xs16[:, k, t * D:(t + 1) * D]
        u_hi = lambda t: xs16[:, 0, t * D:(t + 1) * D]
        u_lo = lambda t: xs16[:, 1, t * D:(t + 1) * D]
        v_hi = lambda t: xs16[:, 2, t * D:(t + 1) * D]
        st16 = stage[:].rearrange("p a b -> p (a b)").bitcast(F16)
        v_lo = lambda t: st16[:, t * D:(t + 1) * D]
        xre = arow[:].rearrange("p a b -> p (a b)").bitcast(F32)
        XB, XT = 8, NT // 8
        SPLITS = ((0, 2), (2, 4), (4, 8), (8, 12), (12, 16))
        NXR = 2
        LAST_TR_AT = 12
        TABLE_AT, FIRST_CORR_AT = 5, 9
        CORR_AT = 1
        POOL_FROM, EDGE_TILE = 9, 10
        u32 = lambda t: xre[:, (2 + t % 2) * D:(3 + t % 2) * D]
        x_again = lambda t: xre[:, (t % NXR) * D:(t % NXR + 1) * D]
        w_raw = [r.rearrange("p (c d) -> p c d", c=DC) for r in (scratch[:], xs[:, 2, 0:2 * DC * D].bitcast(F32))]
        wt_flat = wt[:].rearrange("p a c d -> p (a c d)")
        spare = xs[:, 2, :].bitcast(F32)
        onehot = spare[:, 0:EC * P // 4].bitcast(F8).rearrange("p (k m) -> p k m", m=P)
        adj_rows = spare[:, N:2 * N]
        share = [spare[:, N // 2 + k * D // 2:N // 2 + (k + 1) * D // 2].bitcast(BF16) for k in range(3)]
        xT = scratch[:, 0:2 * D].rearrange("p (a c e) -> p a c e", a=2, c=DC)
        edge_row = spare[:, 0:N // 2].bitcast(BF16)
        masked = xT.rearrange("p a c e -> p (a c) e")
        tp = lambda I: bank[:, 2 * (I % 2):2 * (I % 2) + 2, :].rearrange("p a b -> p (a b)").bitcast(BF16)
        bank_of = lambda n: (2, 3, 4, 5, 6, 0, 1, 7)[n % 8]
        blk = lambda t: slice(t * P, (t + 1) * P)

        xs32 = xs[:].rearrange("p k c -> p (k c)").bitcast(F32)
        kT = xs32[:, 0:DC * N].rearrange("p (c j) -> p c j", c=DC)
        pair_mask = xs32[:, DC * N:(DC + 1) * N]
        floor = xs32[:, (DC + 1) * N:(DC + 2) * N]
        d_score = stage[:, 0, :]
        factor = stage[:, 1, :]
        fT = xre
        v_stage = scratch[:].rearrange("p (t d) -> p t d", t=4)
        gwT = wt_flat[:, 0:N].rearrange("p (c d) -> p c d", c=DC)
        gw_raw = wt_flat[:, N:2 * N].rearrange("p (c d) -> p c d", c=DC)
        qT = wt_flat[:, N:N + D].rearrange("p (c i) -> p c i", c=DC)
        row_hot = wt_flat[:, N + D:N + D + P // 2].bitcast(BF16)
        col_hot = wt_flat[:, N + 2 * D:N + 2 * D + N // 2].bitcast(BF16)
        gx = xj
        gxT = xi[:].rearrange("p (c e) -> p c e", c=DC)

        a_in = [sem("a_in0"), sem("a_in1")]
        x_in = [sem(f"x_in{b}") for b in range(XB)]
        pairs_in = sem("pairs_in")
        w_in = [sem("wq_in"), sem("wk_in")]
        b_in = sem("b_in")
        iota_set = sem("iota_set")
        consts = sem("consts")
        flat_ready = sem("flat_ready")
        adj_e_in = sem("adj_e_in")
        cast_done = sem("cast_done")
        max_diag = sem("max_diag")
        max_mm = sem("max_mm")
        scale_set = sem("scale_set")
        hi_done = sem("hi_done")
        lo_done = sem("lo_done")
        tr_done = sem("tr_done")
        at_act = sem("at_act")
        cols_summed = sem("cols_summed")
        last_sym = sem("last_sym")
        col_sym = sem("col_sym")
        arow_read = sem("arow_read")
        g_mm = sem("g_mm")
        x_half_used = sem("x_half_used")
        g_out = sem("g_out")
        w_tr = sem("w_tr")
        w_out = sem("w_out")
        chain = sem("chain")
        row_live = sem("row_live")
        prefix_mm = sem("prefix_mm")
        order_set = sem("order_set")
        onehot_set = sem("onehot_set")
        compact_mm = sem("compact_mm")
        edge_idx = sem("edge_idx")
        x_edges_in = sem("x_edges_in")
        rows_in = sem("rows_in")
        bc_rhs = sem("bc_rhs")
        bc_mm = sem("bc_mm")
        xt_tr = sem("xt_tr")
        xt_out = sem("xt_out")
        bc_read = sem("bc_read")
        qk_mm = sem("qk_mm")
        score_rhs = sem("score_rhs")
        score_mm = sem("score_mm")
        args_set = sem("args_set")
        exp_done = sem("exp_done")
        pw_set = sem("pw_set")
        z_mm = sem("z_mm")
        table_rhs = sem("table_rhs")
        table_mm = sem("table_mm")
        share_f32 = sem("share_f32")
        share_a = sem("share_a")
        share_p = sem("share_p")
        xr_in = [sem(f"xr_in{k}") for k in range(NXR)]
        corr_mm = sem("corr_mm")
        coef_set = sem("coef_set")
        deg_set = sem("deg_set")
        deg_root = sem("deg_root")
        var1_set = sem("var1_set")
        root1 = sem("root1")
        norm1_set = sem("norm1_set")
        var2_set = sem("var2_set")
        root2 = sem("root2")
        x1_pre = sem("x1_pre")
        x1_done = sem("x1_done")
        u_done = sem("u_done")
        uh_done = sem("uh_done")
        ul_done = sem("ul_done")
        z1_mm = sem("z1_mm")
        vh_done = sem("vh_done")
        vl_done = sem("vl_done")
        y_mm = sem("y_mm")
        y_read = sem("y_read")
        fin_pre = sem("fin_pre")
        fin = sem("fin")
        out_done = sem("out_done")
        gen_start = sem("gen_start")
        gen_w_in = sem("gen_w_in")
        gen_w_tr = sem("gen_w_tr")
        gen_w_out = sem("gen_w_out")
        gen_x_in = sem("gen_x_in")
        gen_x_tr = sem("gen_x_tr")
        gen_x_out = sem("gen_x_out")
        gen_p_mm = sem("gen_p_mm")
        gen_k_out = sem("gen_k_out")
        gen_q_out = sem("gen_q_out")
        gen_a_in = sem("gen_a_in")
        gen_hot = sem("gen_hot")
        gen_pair_mm = sem("gen_pair_mm")
        gen_masks = sem("gen_masks")
        gen_s_mm = sem("gen_s_mm")
        gen_s_read = sem("gen_s_read")
        gen_max = sem("gen_max")
        gen_exp = sem("gen_exp")
        gen_factor = sem("gen_factor")
        gen_f_tr = sem("gen_f_tr")
        gen_f_out = sem("gen_f_out")
        gen_v_in = sem("gen_v_in")
        gen_v_mm = sem("gen_v_mm")
        gen_row = sem("gen_row")
        gen_done = sem("gen_done")
        gen_step = sem("gen_step")

        block = ctx.enter_context(nc.Block())

        @block.sync
        def _(sp):
            def general_loads(sp):
                def load_w(w, n):
                    sp.dma_start(gw_raw, w.rearrange("(c p) d -> p c d", p=P)).then_inc(gen_w_in, 16)
                    sp.wait_ge(gen_w_tr, n)

                sp.wait_ge(gen_start, 1)
                load_w(wk, 1)
                with sp.Fori(0, NT) as J:
                    sp.wait_ge(gen_k_out, J + 1)
                    sp.dma_start(gx[:], x[bass.ds(J * P, P), :]).then_inc(gen_x_in, 16)
                sp.wait_ge(gen_k_out, NT + 1)
                load_w(wq, 2)
                with sp.Fori(0, NT) as I:
                    sp.wait_ge(gen_row, I + 1)
                    sp.dma_start(gx[:], x[bass.ds(I * P, P), :]).then_inc(gen_x_in, 16)
                    sp.dma_start(fT, adj[bass.ds(I * P, P), :]).then_inc(gen_a_in, 16)
                    for q in range(4):
                        sp.wait_ge(gen_v_mm, I * 4 + (q + 1))
                        sp.dma_start(v_stage, x_tiles[:, 4 * q:4 * q + 4, :]).then_inc(gen_v_in, 16)
                sp.wait_ge(gen_done, 1)

            sp.dma_start(pair_i[0:EP], pairs.rearrange("(p k) c -> p k c", p=EP)).then_inc(pairs_in, 16)

            def load_rows(I):
                if I >= 2:
                    sp.wait_ge(cast_done, I - 1)
                sp.dma_start(stage[:, I % 2, :], adj[blk(I), :]).then_inc(a_in[I % 2], 16)

            for b in range(XB):
                sp.dma_start(g[:, XT * b:XT * (b + 1), :], x_tiles[:, XT * b:XT * (b + 1), :]).then_inc(x_in[b], 16)
            load_rows(0)
            load_rows(1)
            for n, w in enumerate((wq, wk)):
                sp.dma_start(w_raw[n], w.rearrange("(c p) d -> p c d", p=P)).then_inc(w_in[n], 16)
            sp.dma_start(bias[0:1, :], bq.rearrange("(a d) -> a d", a=1)).then_inc(b_in, 16)
            sp.dma_start(bias[32:33, :], bk.rearrange("(a d) -> a d", a=1)).then_inc(b_in, 16)
            for I in range(2, NT):
                load_rows(I)
            sp.wait_ge(onehot_set, 2)
            with sp.If(sp.value_load(n_live[0:1, 0:1]) > P):
                general_loads(sp)
            for t in range(NT):
                if t == 0:
                    sp.wait_ge(tr_done, NT - 1)
                    sp.wait_ge(arow_read, NT - 1)
                if t >= NXR:
                    sp.wait_ge(x1_pre, t - NXR + 1)
                sp.dma_start(x_again(t), x_tiles[:, t, :]).then_inc(xr_in[t % NXR], 16)
            for t in range(NT):
                sp.wait_ge(fin, t + 1)
                sp.dma_start(out_tiles[:, t, :], g[:, t, :]).then_inc(out_done, 16)
            sp.wait_ge(out_done, 16 * NT)

        @block.gpsimd
        def _(pool):
            pool.iota(iota_i[:, 0:P], [[1, P]], base=1, channel_multiplier=0).then_inc(iota_set, 1)
            pool.iota(iota_i[:, P:P + 1], [[1, 1]], base=1, channel_multiplier=1).then_inc(iota_set, 1)
            pool.wait_ge(flat_ready, 1)
            for k in range(EC):
                pool.indirect_dma_start(adj_e[0:EP, k:k + 1], None, adj_flat,
                                        bass.IndirectOffsetOnAxis(ap=flat[0:EP, k:k + 1].bitcast(U32), axis=0),
                                        ).then_inc(adj_e_in, 16)
            def symmetrise_columns(I):
                pool.wait_ge(arow_read, I)
                pool.wait_ge(at_act, I + 1)
                pool.tensor_tensor(sym[:, 0:I, blk(I)], sym[:, 0:I, blk(I)], at[:, 0:I, blk(I)], ALU.add,
                                   saturate=False).then_inc(col_sym, 1)

            for I in range(POOL_FROM, EDGE_TILE):
                symmetrise_columns(I)
            pool.wait_ge(edge_idx, 1)
            for n, (dst, src) in enumerate(((xi, x), (xj, x))):
                pool.indirect_dma_start(dst[:], None, src,
                                        bass.IndirectOffsetOnAxis(ap=e_idx[:, n:n + 1].bitcast(U32), axis=0),
                                        ).then_inc(x_edges_in, 16)
            pool.indirect_dma_start(adj_rows, None, adj,
                                    bass.IndirectOffsetOnAxis(ap=e_idx[:, 0:1].bitcast(U32), axis=0),
                                    ).then_inc(rows_in, 16)
            for I in range(EDGE_TILE, NT - 1):
                symmetrise_columns(I)
            for k in range(2):
                pool.wait_ge(share_a, k + 1)
                dst = xi[:] if k == 0 else share[2]
                pool.tensor_tensor(dst, xi[:], share[k], ALU.subtract).then_inc(share_p, 1)
            L = NT - 1
            pool.wait_ge(cast_done, NT)
            pool.wait_ge(at_act, NT)
            pool.wait_ge(arow_read, NT)
            pool.wait_ge(deg_set, 1)
            pool.tensor_tensor(sym[:, L, :], arow[:, L % 2, :], at[:, L, :], ALU.add,
                               saturate=False).then_inc(last_sym, 1)
            pool.tensor_tensor(sym[:, 0:L, blk(L)], sym[:, 0:L, blk(L)], at[:, 0:L, blk(L)], ALU.add,
                               saturate=False).then_inc(last_sym, 1)
            pool.wait_ge(last_sym, 1)
            pool.tensor_tensor(sym[:, L, blk(L)], sym[:, L, blk(L)], ident2[:], ALU.add,
                               saturate=False).then_inc(last_sym, 1)
            for t in range(NT):
                pool.wait_ge(uh_done, t + 1)
                pool.tensor_tensor(u_lo(t), u32(t), u_hi(t), ALU.subtract).then_inc(ul_done, 1)

        @block.tensor
        def _(pe):
            def transposes(I):
                pe.wait_ge(cast_done, I + 1)
                if I >= 2:
                    pe.wait_ge(cols_summed, I - 1)
                    pe.wait_ge(at_act, I - 1)
                for J in range(NT):
                    last = pe.transpose(tp(I)[:, blk(J)], arow[:, I % 2, blk(J)], identb[:])
                last.then_inc(tr_done, 1)

            def adj_x(I, J0=0, J1=NT):
                if J0 == 0:
                    pe.wait_ge(at_act, I + 1)
                    if I >= 2:
                        pe.wait_ge(g_out, I - 1)
                for J in range(J0, J1):
                    for k in range(2):
                        last = pe.matmul(bank[:, 4 + I % 2, :], at[:, J, blk(I)], xpart(k, J),
                                         start=(J == 0 and k == 0), stop=(J == NT - 1 and k == 1))
                if J1 == NT:
                    last.then_inc(g_mm, 1)
                elif I == NT - 1 and J1 == NT // 2:
                    last.then_inc(x_half_used, 1)

            def w_transposes(n):
                pe.wait_ge(w_in[n // 2], 16)
                for c in range(2):
                    if n:
                        pe.wait_ge(w_out, 2 * n + c - 1)
                    for o in range(DC):
                        last = pe.transpose(bank[:, 6 + c, blk(o)], w_raw[n // 2][:, o, blk(2 * (n % 2) + c)], ident[:])
                    last.then_inc(w_tr, 1)

            def edge_prefix():
                pe.wait_ge(row_live, 1)
                pe.wait_ge(w_out, 8)
                pe.matmul(bank[0:EP, 6, 0:1], before[0:EP, 0:EP], e_sm[0:EP, TOT:TOT + 1], start=True, stop=True)
                pe.matmul(bank[:, 6, 1:2], ones[0:EP, :], e_sm[0:EP, TOT:TOT + 1],
                          start=True, stop=True).then_inc(prefix_mm, 1)

            def edge_compact():
                pe.wait_ge(onehot_set, 2)
                for k in range(EC):
                    last = pe.matmul(bank[:, 7, 0:3], onehot[0:EP, k, :], pair_h[0:EP, k, :],
                                     start=(k == 0), stop=(k == EC - 1))
                last.then_inc(compact_mm, 1)

            def edge_broadcast():
                pe.wait_ge(bc_rhs, 1)
                pe.matmul(bank[:, 6, 0:P], ones[:], tmp[:], start=True, stop=True)
                pe.matmul(bank[:, 6, P:2 * P], ones[:], other_row[:], start=True, stop=True).then_inc(bc_mm, 1)

            def edge_x_transposes():
                pe.wait_ge(x_edges_in, 32)
                pe.wait_ge(w_out, 8)
                pe.wait_ge(bc_read, 1)
                for n, src in enumerate((xi, xj)):
                    for c in range(DC):
                        last = pe.transpose(bank[:, 6 + n, blk(c)], src[:, blk(c)], ident[:])
                last.then_inc(xt_tr, 1)

            def edge_project():
                pe.wait_ge(xt_out, 2)
                pe.wait_ge(b_in, 32)
                for n in range(2):
                    for c in range(DC):
                        pe.matmul(bank[:, 6 + n, :], xT[:, n, c, :], wt[:, n, c, :], start=(c == 0), stop=False)
                    last = pe.matmul(bank[:, 6 + n, :], ones[32 * n:32 * n + 1, :], bias[32 * n:32 * n + 1, :], start=False, stop=True)
                last.then_inc(qk_mm, 1)

            def edge_score_rows():
                pe.wait_ge(score_rhs, 1)
                for n in range(2):
                    last = pe.matmul(bank[:, 6 + n, :], ones[:],
                                     xT[:, n, :, :].rearrange("p c e -> p (c e)"), start=True, stop=True)
                last.then_inc(score_mm, 1)

            def edge_sums():
                pe.wait_ge(pw_set, 1)
                pe.matmul(bank[:, 6, 0:HEADS + 1], same_row[:], pw[:], start=True, stop=True).then_inc(z_mm, 1)

            def edge_table():
                pe.wait_ge(table_rhs, 1)
                for t in range(NT):
                    for k in range(3):
                        last = pe.matmul(bank[:, 7, 4 * t:4 * t + 3], edge_row[:, blk(t)], trow_b[:, k, 0:3],
                                         start=(k == 0), stop=(k == 2))
                last.then_inc(table_mm, 1)

            def correct(t):
                if t == 2:
                    pe.wait_ge(coef_set, 1)
                if t == 0:
                    pe.wait_ge(at_act, NT)
                    pe.wait_ge(cols_summed, NT)
                    pe.wait_ge(share_a, 2)
                    pe.wait_ge(share_p, 2)
                if t >= 3:
                    pe.wait_ge(x1_pre, t - 2)
                for k in range(3):
                    last = pe.matmul(bank[:, (0, 1, 7)[t % 3], :], edge_row[:, blk(t)], share[k],
                                     start=(k == 0), stop=(k == 2))
                last.then_inc(corr_mm, 1)

            pe.wait_ge(consts, 1)
            pe.wait_ge(max_diag, 1)
            pe.matmul(bank[:, 6, 0:P], ones[:], same_row[:], start=True, stop=True).then_inc(max_mm, 1)
            transposes(0)
            for b, (J0, J1) in enumerate(SPLITS):
                pe.wait_ge(hi_done, b + 1)
                pe.wait_ge(lo_done, b + 1)
                adj_x(0, J0, J1)
                if J1 == 12:
                    transposes(1)
            adj_x(1)
            transposes(2)
            transposes(3)
            w_transposes(0)
            for I in range(2, NT):
                if I == NT - 1:
                    adj_x(I, 0, TABLE_AT)
                    edge_table()
                    adj_x(I, TABLE_AT, NT // 2)
                    adj_x(I, NT // 2, FIRST_CORR_AT)
                    for t in range(3):
                        correct(t)
                    adj_x(I, FIRST_CORR_AT, NT)
                    continue
                adj_x(I, 0, NT // 2)
                if I in (3, 4, 5):
                    w_transposes(I - 2)
                if I == 7:
                    edge_prefix()
                if I == 10:
                    edge_broadcast()
                if I == 11:
                    edge_x_transposes()
                if I == 13:
                    edge_score_rows()
                done = NT // 2
                if I == 13:
                    done = LAST_TR_AT
                    adj_x(I, NT // 2, done)
                    transposes(NT - 1)
                if I == 14:
                    edge_sums()
                adj_x(I, done, NT)
                if I + 3 < NT:
                    transposes(I + 2)
                if I == 9:
                    edge_compact()
                if I == 11:
                    edge_project()

            def general_products(pe):
                def w_transposed(n):
                    pe.wait_ge(gen_w_in, 16 * n)
                    for c in range(DC):
                        for o in range(DC):
                            last = pe.transpose(bank[:, c, blk(o)], gw_raw[:, o, blk(c)], ident[:])
                    last.then_inc(gen_w_tr, 1)
                    pe.wait_ge(gen_w_out, n)

                def project(n, bias_row):
                    pe.wait_ge(gen_x_in, n * 16)
                    for c in range(DC):
                        last = pe.transpose(bank[:, 0, blk(c)], gx[:, blk(c)], ident[:])
                    last.then_inc(gen_x_tr, 1)
                    pe.wait_ge(gen_x_out, n)
                    for o in range(DC):
                        for c in range(DC):
                            pe.matmul(bank[:, 1, blk(o)], gwT[:, c, blk(o)], gxT[:, c, :], start=(c == 0), stop=False)
                        last = pe.matmul(bank[:, 1, blk(o)], bias[bias_row:bias_row + 1, blk(o)],
                                         ones[bias_row:bias_row + 1, :], start=False, stop=True)
                    last.then_inc(gen_p_mm, 1)

                def pair_product(n, start, stop):
                    pe.wait_ge(gen_hot, n)
                    for c in range(4):
                        last = pe.matmul(bank[:, 2 + c, :], row_hot[0:EP, :], col_hot[0:EP, c * 512:(c + 1) * 512],
                                         start=start, stop=stop)
                    last.then_inc(gen_pair_mm, 1)

                pe.wait_ge(gen_start, 1)
                pe.wait_ge(g_out, NT - 1)
                w_transposed(1)
                with pe.Fori(0, NT) as J:
                    pe.wait_ge(gen_k_out, J + 1)
                    project(J + 1, 32)
                pe.wait_ge(gen_k_out, NT + 1)
                w_transposed(2)
                pe.sem_inc(gen_v_mm, 1)
                with pe.Fori(0, NT) as I:
                    pe.wait_ge(gen_row, I + 1)
                    project(I + (NT + 1), 0)
                    pair_product(I * EC + 1, True, False)
                    with pe.Fori(1, EC - 1) as k:
                        pair_product(I * EC + k + 1, False, False)
                    pair_product(I * EC + EC, False, True)
                    pe.wait_ge(gen_q_out, I + 1)
                    pe.wait_ge(gen_masks, I + 1)
                    for h in range(HEADS):
                        if h:
                            pe.wait_ge(gen_s_read, I * HEADS + h)
                        half = slice(DK * (h % 2), DK * (h % 2) + DK)
                        for c in range(4):
                            last = pe.matmul(bank[:, 2 + c, :], qT[half, h // 2, :],
                                             kT[half, h // 2, c * 512:(c + 1) * 512], start=True, stop=True)
                        last.then_inc(gen_s_mm, 1)
                    pe.wait_ge(gen_factor, I + 1)
                    for J in range(NT):
                        last = pe.transpose(bank[:, 2 + J // 4, blk(J % 4)], factor[:, blk(J)], ident[:])
                    last.then_inc(gen_f_tr, 1)
                    pe.wait_ge(gen_f_out, I + 1)
                    for q in range(4):
                        pe.wait_ge(gen_v_in, I * 64 + 16 * (q + 1))
                        for r in range(4):
                            J = 4 * q + r
                            last = pe.matmul(bank[:, 6, :], fT[:, blk(J)], v_stage[:, r, :],
                                             start=(J == 0), stop=(J == NT - 1))
                        last.then_inc(gen_v_mm, 1)
                pe.wait_ge(gen_done, 1)

            with pe.If(pe.value_load(n_live[0:1, 0:1]) > P):
                general_products(pe)

            pe.wait_ge(g_out, NT - 1)
            correct(3)
            for J in range(NT):
                if J == NT - 1:
                    pe.wait_ge(last_sym, 3)
                    pe.wait_ge(col_sym, NT - 1 - POOL_FROM)
                pe.wait_ge(uh_done, J + 1)
                pe.wait_ge(ul_done, J + 1)
                for m in range(KOUT):
                    if m == CORR_AT and J + 4 < NT:
                        correct(J + 4)
                    if J == 0 and bank_of(m) == 4 + (NT - 1) % 2:
                        pe.wait_ge(g_out, NT)
                    for k, u in enumerate((u_hi, u_lo)):
                        last = pe.matmul(bank[:, bank_of(m), :], sym[:, J, blk(m)], u(J),
                                         start=(J == 0 and k == 0), stop=(J == NT - 1 and k == 1))
                    if J == NT - 1:
                        last.then_inc(z1_mm, 1)

            def free_bank(n, eng):
                if n < 8:
                    eng.wait_ge(x1_pre, NT)
                elif n < NT + 8:
                    eng.wait_ge(vl_done, n - 7)
                else:
                    eng.wait_ge(y_read, n - NT - 7)

            for n in range(KOUT, NT):
                free_bank(n, pe)
                for J in range(NT):
                    for k, u in enumerate((u_hi, u_lo)):
                        last = pe.matmul(bank[:, bank_of(n), :], sym[:, J, blk(n)], u(J),
                                         start=(J == 0 and k == 0), stop=(J == NT - 1 and k == 1))
                last.then_inc(z1_mm, 1)

            def adj_v(I, J0, J1):
                for J in range(J0, J1):
                    pe.wait_ge(vh_done, J + 1)
                    pe.wait_ge(vl_done, J + 1)
                    for k, v in enumerate((v_hi, v_lo)):
                        last = pe.matmul(bank[:, bank_of(NT + I), :], at[:, J, blk(I)], v(J),
                                         start=(J == 0 and k == 0), stop=(J == NT - 1 and k == 1))
                return last

            free_bank(NT, pe)
            adj_v(0, 0, NT - 1)
            free_bank(NT + 1, pe)
            adj_v(1, 0, NT - 1)
            adj_v(0, NT - 1, NT).then_inc(y_mm, 1)
            adj_v(1, NT - 1, NT).then_inc(y_mm, 1)
            for I in range(2, NT):
                free_bank(NT + I, pe)
                adj_v(I, 0, NT).then_inc(y_mm, 1)

        @block.scalar
        def _(act):
            def cast_rows(I):
                act.wait_ge(a_in[I % 2], 16 * (I // 2 + 1))
                if I >= 2:
                    act.wait_ge(tr_done, I - 1)
                    act.wait_ge(arow_read, I - 1)
                act.activation(arow[:, I % 2, :], stage[:, I % 2, :], ACT.Copy,
                               accum_out=row_sum[:, I:I + 1]).then_inc(cast_done, 1)

            def save_at(I):
                act.wait_ge(tr_done, I + 1)
                act.copy(at[:, :, blk(I)], tp(I).rearrange("p (j i) -> p j i", i=P),
                         saturate=False).then_inc(at_act, 1)

            def split_x(b):
                J0, J1 = SPLITS[b]
                src = g[:, J0:J1, :].rearrange("p t d -> p (t d)")
                if b == 0:
                    act.wait_ge(scale_set, 1)
                act.activation(xs16[:, 0, J0 * D:J1 * D], src, ACT.Copy, scale=xscale[:, 5:6]).then_inc(hi_done, 1)

            cast_rows(0)
            split_x(0)
            split_x(1)
            save_at(0)
            split_x(2)
            split_x(3)
            cast_rows(1)
            split_x(4)
            save_at(1)
            cast_rows(2)
            def save_g(I):
                act.wait_ge(g_mm, I + 1)
                if I == 0:
                    act.wait_ge(lo_done, len(SPLITS))
                act.copy(g[:, I, :], bank[:, 4 + I % 2, :]).then_inc(g_out, 1)

            def save_wt(n):
                for c in range(2):
                    act.wait_ge(w_tr, 2 * n + c + 1)
                    act.copy(wt[:, n // 2, 2 * (n % 2) + c, :], bank[:, 6 + c, :]).then_inc(w_out, 1)

            for I in range(NT):
                if I in (3, 4, 5):
                    save_wt(I - 2)
                if I == 11:
                    act.wait_ge(xt_tr, 1)
                    for n in range(2):
                        act.copy(xT[:, n, :, :].rearrange("p c e -> p (c e)"), bank[:, 6 + n, :]).then_inc(xt_out, 1)
                if I == 0:
                    cast_rows(3)
                if I + 2 < NT:
                    save_at(I + 2)
                if 3 < I + 3 < NT:
                    cast_rows(I + 3)
                if I < NT - 1 and I != 13:
                    save_g(I)
                if I == 1:
                    save_wt(0)
                if I == 13:
                    act.wait_ge(args_set, 1)
                    act.activation(exps[:], args[:], ACT.Exp).then_inc(exp_done, 1)
                    act.wait_ge(deg_set, 1)
                    act.sqrt(rt[:, T3, :], deg[:]).then_inc(deg_root, 1)
                    save_g(I)
                    act.wait_ge(share_f32, 1)
                    act.copy(share[0], xi[:]).then_inc(share_a, 1)
                    act.wait_ge(share_p, 1)
                    act.copy(share[1], xi[:]).then_inc(share_a, 1)
            with act.If(act.value_load(n_live[0:1, 0:1]) > P):
                with act.Fori(0, NT) as I:
                    for h in range(HEADS):
                        act.wait_ge(gen_max, I * HEADS + (h + 1))
                        act.activation(d_score, d_score, ACT.Exp, bias=mv[:, 0, 1:2],
                                       accum_out=mv[:, 0, 2:3]).then_inc(gen_exp, 1)
            act.wait_ge(coef_set, 1)
            act.sqrt(junk_root[:], eps[:])
            for t in range(NT + 1):
                if t < NT:
                    act.wait_ge(var1_set, t + 1)
                    act.activation(mv[:, t % 4, 3:4], mv[:, t % 4, 1:2], ACT.Sqrt, bias=eps[:, 0:1]).then_inc(root1, 1)
                if t:
                    m = mv[:, (t - 1) % 4, :]
                    act.wait_ge(norm1_set, t)
                    act.activation(g[:, t - 1, :], g[:, t - 1, :], ACT.Identity, bias=m[:, 5:6],
                                   scale=m[:, 4:5]).then_inc(x1_done, 1)
                    if t == 1:
                        act.wait_ge(tr_done, NT)
                        act.wait_ge(arow_read, NT)
                        act.wait_ge(last_sym, 1)
                        act.wait_ge(x_half_used, 1)
                    if t == NT // 2 + 1:
                        act.wait_ge(g_mm, NT)
                    if t >= 3:
                        act.wait_ge(ul_done, t - 2)
                    act.wait_ge(x1_done, t)
                    act.activation(u32(t - 1), g[:, t - 1, :], ACT.Copy,
                                   scale=rt[:, SDINV, t - 1:t]).then_inc(u_done, 1)
                    act.wait_ge(u_done, t)
                    act.copy(u_hi(t - 1), u32(t - 1)).then_inc(uh_done, 1)
                if t == 1:
                    save_g(NT - 1)
            for t in range(NT):
                act.wait_ge(z1_mm, t + 1)
                act.activation(v_hi(t), bank[:, bank_of(t), :], ACT.Copy,
                               scale=rt[:, SCALE_V, t:t + 1]).then_inc(vh_done, 1)
            for t in range(NT + 1):
                if t < NT:
                    act.wait_ge(var2_set, t + 1)
                    act.activation(mv[:, t % 4, 3:4], mv[:, t % 4, 1:2], ACT.Sqrt, bias=eps[:, 0:1]).then_inc(root2, 1)
                if t:
                    act.wait_ge(fin_pre, t)
                    act.activation(g[:, t - 1, :], g[:, t - 1, :], ACT.Identity, bias=mv[:, (t - 1) % 4, 5:6],
                                   scale=mv[:, (t - 1) % 4, 4:5]).then_inc(fin, 1)

        @block.vector
        def _(dve):
            links = [0]

            def link(ins):
                links[0] += 1
                ins.then_inc(chain, 1)
                dve.wait_ge(chain, links[0])

            def mark(ins):
                links[0] += 1
                ins.then_inc(chain, 1)
                return links[0]

            mark(dve.memset(ones[:], 1.0))
            mark(dve.memset(eps[:], LN_EPS))
            mark(dve.memset(col_part[:], 0.0))
            mark(dve.memset(pair_h[:], 1.0))
            dve.wait_ge(iota_set, 2)
            link(dve.tensor_copy(iota[:], iota_i))
            link(dve.tensor_scalar(identb[:], iota[:, 0:P], iota[:, P:P + 1], None, ALU.is_equal))
            mark(dve.tensor_scalar(ident[:], iota[:, 0:P], iota[:, P:P + 1], None, ALU.is_equal))
            mark(dve.tensor_scalar(ident2[:], identb[:], 2.0, None, ALU.mult))
            dve.tensor_scalar(before[:], iota[:, 0:P], iota[:, P:P + 1], None, ALU.is_gt).then_inc(consts, 1)
            dve.wait_ge(pairs_in, 16)
            link(dve.tensor_copy(pair_f[0:EP], pair_i[0:EP]))
            dve.scalar_tensor_tensor(flat[0:EP], pair_f[0:EP, :, 0], float(N), pair_f[0:EP, :, 1],
                                     ALU.mult, ALU.add).then_inc(flat_ready, 1)
            dve.tensor_copy(pair_h[0:EP, :, 0:2], pair_f[0:EP]).then_inc(flat_ready, 1)

            def column_sums(I):
                dve.tensor_reduce(col_part[:, :, I], tp(I).rearrange("p (j i) -> p j i", i=P),
                                  AX, ALU.add).then_inc(cols_summed, 1)

            def symmetrise(I):
                w = (I + 1) * P
                dve.wait_ge(cast_done, I + 1)
                dve.wait_ge(at_act, I + 1)
                column_sums(I)
                if I == NT - 1:
                    row_exp()
                    row_degrees()
                ins = dve.scalar_tensor_tensor(junk[:], arow[:, I % 2, blk(I)], 1.0, identb[:], ALU.mult, ALU.mult,
                                               accum_out=diag[:, I:I + 1])
                if I == NT - 1:
                    ins.then_inc(arow_read, 1)
                    return
                mark(dve.tensor_copy(sym[:, I, w:N], arow[:, I % 2, w:N], saturate=False))
                dve.tensor_tensor(sym[:, I, 0:w], arow[:, I % 2, 0:w], at[:, I, 0:w], ALU.add,
                                  saturate=False).then_inc(arow_read, 1)
                dve.wait_ge(arow_read, I + 1)
                link(dve.tensor_tensor(sym[:, I, blk(I)], sym[:, I, blk(I)], ident2[:], ALU.add, saturate=False))
                if 0 < I < POOL_FROM:
                    mark(dve.tensor_tensor(sym[:, 0:I, blk(I)], sym[:, 0:I, blk(I)], at[:, 0:I, blk(I)], ALU.add,
                                           saturate=False))

            for b in range(XB):
                dve.wait_ge(x_in[b], 16)
                last = mark(dve.tensor_reduce(xscale[:, 8 + b:9 + b],
                                              g[:, XT * b:XT * (b + 1), :].rearrange("p t d -> p (t d)"),
                                              AX, ALU.max, apply_absolute_value=True))
            dve.wait_ge(chain, last)
            link(dve.tensor_reduce(xscale[:, 4:5], xscale[:, 8:8 + XB], AX, ALU.max))
            dve.tensor_scalar(same_row[:], ident[:], xscale[:, 4:5], None, ALU.mult).then_inc(max_diag, 1)
            dve.wait_ge(max_mm, 1)
            link(dve.tensor_reduce(xscale[:, 4:5], bank[:, 6, 0:P], AX, ALU.max))
            link(dve.tensor_scalar(xscale_i[:, 4:5], xscale_i[:, 4:5], 0x7F800000, None, ALU.bitwise_and))
            link(dve.tensor_scalar(xscale_i[:, 5:6], xscale_i[:, 4:5], -1.0, float((254 + 10) << 23),
                                   ALU.mult, ALU.add))
            dve.tensor_scalar(xscale_i[:, 6:7], xscale_i[:, 5:6], -1.0, float(254 << 23),
                              ALU.mult, ALU.add).then_inc(scale_set, 1)

            def split_x(b):
                J0, J1 = SPLITS[b]
                cols = slice(J0 * D, J1 * D)
                src = g[:, J0:J1, :].rearrange("p t d -> p (t d)")
                dve.wait_ge(hi_done, b + 1)
                dve.scalar_tensor_tensor(xs16[:, 1, cols], src, xscale[:, 5:6], xs16[:, 0, cols],
                                         ALU.mult, ALU.subtract).then_inc(lo_done, 1)

            for b in range(len(SPLITS)):
                split_x(b)
            symmetrise(0)
            symmetrise(1)

            def edge_live():
                dve.wait_ge(adj_e_in, 16 * EC)
                link(dve.tensor_tensor(order[0:EP], pair_f[0:EP, :, 0], pair_f[0:EP, :, 1], ALU.not_equal))
                link(dve.scalar_tensor_tensor(live[0:EP], adj_e[0:EP], 1.0, order[0:EP], ALU.is_equal, ALU.mult))
                dve.tensor_reduce(e_sm[0:EP, TOT:TOT + 1], live[0:EP], AX, ALU.add).then_inc(row_live, 1)

            def edge_order():
                dve.wait_ge(prefix_mm, 1)
                mark(dve.tensor_copy(n_live[:], bank[:, 6, 1:2]))
                link(dve.tensor_copy(e_sm[0:EP, W1:W1 + 1], bank[0:EP, 6, 0:1]))
                link(dve.tensor_tensor_scan(order[0:EP], ones[0:EP, 0:EC], live[0:EP], e_sm[0:EP, W1:W1 + 1],
                                            ALU.mult, ALU.add))
                dve.tensor_tensor(order[0:EP], order[0:EP], live[0:EP], ALU.mult).then_inc(order_set, 1)

            def edge_onehot(half):
                dve.wait_ge(order_set, 1)
                w = EC // 2
                cols = slice(half * w, half * w + w)
                dve.tensor_tensor(onehot[0:EP, cols, :],
                                  order[0:EP, cols].rearrange("p (k o) -> p k o", o=1).broadcast_to((EP, w, P)),
                                  iota[0:EP, 0:P].rearrange("p (o m) -> p o m", o=1).broadcast_to((EP, w, P)),
                                  ALU.is_equal, saturate=False).then_inc(onehot_set, 1)

            def edge_list():
                dve.wait_ge(compact_mm, 1)
                link(dve.tensor_copy(e_sm[:, 0:3], bank[:, 7, 0:3]))
                dve.tensor_copy(e_idx[:], e_sm[:, 0:2]).then_inc(edge_idx, 1)
                link(dve.scalar_tensor_tensor(ec(IV), ec(I_), -1.0, ec(V_), ALU.add, ALU.add))
                mark(dve.tensor_scalar(ec(EMPTY), ec(V_), -1.0, 1.0, ALU.mult, ALU.add))
                link(dve.scalar_tensor_tensor(ec(FV), ec(I_), float(N), ec(J_), ALU.mult, ALU.add))
                link(dve.scalar_tensor_tensor(ec(FV), ec(FV), -1.0, ec(V_), ALU.add, ALU.add))
                mark(dve.tensor_scalar(tmp[:], ident[:], ec(IV), None, ALU.mult))
                dve.tensor_scalar(other_row[:], ident[:], ec(FV), None, ALU.mult).then_inc(bc_rhs, 1)

            def edge_masks():
                dve.wait_ge(bc_mm, 1)
                link(dve.tensor_scalar(same_row[:], bank[:, 6, P:2 * P], ec(FV), 0.0, ALU.is_equal, ALU.add,
                                       accum_out=ec(MULT)))
                link(dve.tensor_scalar(same_row[:], bank[:, 6, 0:P], ec(IV), 0.0, ALU.is_equal, ALU.add,
                                       accum_out=ec(SAME)))
                dve.tensor_scalar(other_row[:], same_row[:], -1.0, BIG, ALU.add, ALU.mult).then_inc(bc_read, 1)
                link(dve.reciprocal(e_sm[:, MULT:SAME + 1], e_sm[:, MULT:SAME + 1]))
                link(dve.tensor_scalar(e_sm[:, MULT:SAME + 1], e_sm[:, MULT:SAME + 1], ec(V_), None, ALU.mult))


            def edge_scores():
                dve.wait_ge(qk_mm, 1)
                link(dve.tensor_copy(xi[:], bank[:, 6, :]))
                link(dve.tensor_tensor(xi[:], xi[:], bank[:, 7, :], ALU.mult))
                link(dve.tensor_reduce(score[:], xi[:].rearrange("p (h d) -> p h d", h=HEADS), AX, ALU.add))
                link(dve.tensor_scalar(score[:], score[:], float(DK) ** -0.5, None, ALU.mult))
                dve.tensor_tensor(masked, score[:].rearrange("p (h o) -> p h o", o=1).broadcast_to((P, HEADS, P)),
                                  ident[:].rearrange("p (o m) -> p o m", o=1).broadcast_to((P, HEADS, P)),
                                  ALU.mult).then_inc(score_rhs, 1)

            def edge_counts():
                dve.wait_ge(compact_mm, 1)
                link(dve.tensor_scalar(rt[:, T1, :], iota[:, 0:NT], -float(P), ec(I_), ALU.mult, ALU.add))
                link(dve.tensor_scalar(rt[:, T1, :], rt[:, T1, :], float(P) + 1.0, None, ALU.add))
                link(dve.tensor_tensor(edge_row.rearrange("p (t m) -> p t m", m=P),
                                       rt[:, T1, :].rearrange("p (t o) -> p t o", o=1).broadcast_to((P, NT, P)),
                                       iota[:, 0:P].rearrange("p (o m) -> p o m", o=1).broadcast_to((P, NT, P)),
                                       ALU.is_equal))
                dve.wait_ge(rows_in, 16)
                mark(dve.scalar_tensor_tensor(adj_rows, edge_row, 1.0, adj_rows, ALU.subtract, ALU.mult,
                                              accum_out=ec(CNT)))

            def edge_max():
                dve.wait_ge(score_mm, 1)
                link(dve.tensor_tensor(masked, bank[:, 6:8, :].rearrange("p a (c e) -> p (a c) e", e=P),
                                       other_row[:].rearrange("p (o m) -> p o m", o=1).broadcast_to((P, HEADS, P)),
                                       ALU.add))
                link(dve.tensor_reduce(zz[:, 0, :], masked, AX, ALU.max))
                link(dve.tensor_scalar(args[:, 0, :], zz[:, 0, :], SELF_SCORE, -1.0, ALU.max, ALU.mult))
                mark(dve.tensor_scalar(args[:, 1, :], args[:, 0, :], SELF_SCORE, None, ALU.add))
                dve.tensor_tensor(args[:, 2, :], args[:, 0, :], score[:], ALU.add).then_inc(args_set, 1)

            def row_exp():
                dve.wait_ge(exp_done, 1)
                mark(dve.tensor_scalar(pw[:, 0:HEADS], exps[:, 2, :], ec(MULT), None, ALU.mult))
                dve.tensor_copy(pw[:, HEADS:HEADS + 1], ec(MULT)).then_inc(pw_set, 1)

            def in_three(v, parts, done):
                link(dve.tensor_copy(parts[0], v))
                link(dve.tensor_tensor(v, v, parts[0], ALU.subtract))
                link(dve.tensor_copy(parts[1], v))
                dve.tensor_tensor(parts[2], v, parts[1], ALU.subtract).then_inc(done, 1)

            def edge_weights():
                dve.wait_ge(z_mm, 1)
                link(dve.scalar_tensor_tensor(ec(CNT), ec(CNT), -1.0, bank[:, 6, HEADS:HEADS + 1],
                                              ALU.mult, ALU.subtract))
                link(dve.scalar_tensor_tensor(zz[:, 1, :], exps[:, 0, :], ec(CNT), exps[:, 1, :], ALU.mult, ALU.add))
                link(dve.tensor_tensor(zz[:, 1, :], zz[:, 1, :], bank[:, 6, 0:HEADS], ALU.add))
                link(dve.tensor_scalar(zz[:, 1, :], zz[:, 1, :], ec(EMPTY), float(HEADS), ALU.add, ALU.mult))
                link(dve.reciprocal(zz[:, 1, :], zz[:, 1, :]))
                link(dve.tensor_tensor(args[:], exps[:], zz[:, 1:2, :].broadcast_to((P, 3, HEADS)), ALU.mult))
                link(dve.tensor_reduce(e_sm[:, W1:W3 + 1], args[:], AX, ALU.add))
                link(dve.tensor_tensor(ec(W3), ec(W3), ec(W1), ALU.subtract))
                link(dve.tensor_tensor(ec(W3), ec(W3), ec(MULT), ALU.mult))
                dve.tensor_scalar(xi[:], xj[:], ec(W3), None, ALU.mult).then_inc(share_f32, 1)
                mark(dve.tensor_copy(trow[:, 0:1], ec(SAME)))
                link(dve.tensor_scalar(trow[:, 1:3], e_sm[:, W1:W2 + 1], ec(SAME), None, ALU.mult))
                in_three(trow[:, 0:3], [trow_b[:, k, 0:3] for k in range(3)], table_rhs)

            def inverse_root(v, root, out, w):
                link(dve.reciprocal(out, root))
                link(dve.tensor_tensor(w, out, out, ALU.mult))
                link(dve.tensor_tensor(w, w, v, ALU.mult))
                link(dve.tensor_scalar(w, w, -0.5, 1.5, ALU.mult, ALU.add))
                link(dve.tensor_tensor(out, out, w, ALU.mult))

            def row_degrees():
                dve.wait_ge(cols_summed, NT)
                r = lambda k: rt[:, k, :]
                link(dve.tensor_reduce(r(T2), col_part[:], AX, ALU.add))
                link(dve.tensor_tensor(r(T2), r(T2), row_sum[:], ALU.add))
                dve.tensor_scalar(deg[:], r(T2), 0.5, 1.0, ALU.mult, ALU.add).then_inc(deg_set, 1)

            def row_scales():
                dve.wait_ge(arow_read, NT)
                r = lambda k: rt[:, k, :]
                em0 = float(np_exp(-SELF_SCORE))
                link(dve.tensor_tensor(r(T1), row_sum[:], diag[:], ALU.subtract))
                link(dve.tensor_scalar(r(T1), r(T1), em0, 1.0, ALU.mult, ALU.add))
                link(dve.reciprocal(r(T1), r(T1)))
                dve.wait_ge(deg_root, 1)
                inverse_root(deg[:], r(T3), r(T2), r(SDINV))
                mark(dve.tensor_scalar(r(SDINV), r(T2), U_SCALE, None, ALU.mult))
                link(dve.tensor_scalar(r(SCALE_V), r(T2), 0.5 * V_SCALE / U_SCALE, None, ALU.mult))

            def row_coefficients():
                tab = bank[:, 7, 0:4 * NT].rearrange("p (t c) -> p c t", c=4)
                em0 = float(np_exp(-SELF_SCORE))
                r = lambda k: rt[:, k, :]
                dve.wait_ge(table_mm, 1)
                link(dve.tensor_scalar(r(T3), tab[:, 0, :], -1.0, 1.0, ALU.mult, ALU.add))
                link(dve.tensor_tensor(r(T3), r(T3), r(T1), ALU.mult))
                mark(dve.scalar_tensor_tensor(r(ALPHA), r(T3), em0, tab[:, 1, :], ALU.mult, ALU.add))
                ins = dve.tensor_tensor(r(BETA), r(T3), tab[:, 2, :], ALU.add)
                ins.then_inc(coef_set, 1)
                dve.wait_ge(coef_set, 1)
                link(dve.tensor_tensor(r(T3), r(ALPHA), diag[:], ALU.mult))
                mark(dve.tensor_scalar(r(ALPHA), r(ALPHA), xscale[:, 6:7], None, ALU.mult))
                link(dve.scalar_tensor_tensor(r(BETA), r(BETA), 1.0, r(T3), ALU.add, ALU.subtract))

            for I in range(NT):
                if I + 3 < NT:
                    symmetrise(I + 2)
                if I == 5:
                    edge_live()
                if I == 6:
                    edge_order()
                    edge_onehot(0)
                if I == 7:
                    edge_onehot(1)
                if I == 8:
                    edge_list()
                if I == 9:
                    edge_masks()
                if I == 10:
                    edge_counts()
                if I == 11:
                    edge_scores()
                if I == 12:
                    edge_max()
                if I == 13:
                    symmetrise(NT - 1)
                    edge_weights()
                    row_scales()
            row_coefficients()

            def general_path(dve):
                shift, tile_no = mv[:, 1, 0:1], mv[:, 1, 1:2]

                def step(ins):
                    ins.then_inc(gen_step, 1)
                    dve.wait_ge(gen_step, 1)
                    dve.sem_clear(gen_step)

                def w_out(n):
                    dve.wait_ge(gen_w_tr, n)
                    dve.tensor_copy(gwT.rearrange("p c d -> p (c d)"),
                                    bank[:, 0:4, :].rearrange("p a b -> p (a b)")).then_inc(gen_w_out, 1)

                def x_out(n):
                    dve.wait_ge(gen_x_tr, n)
                    dve.tensor_copy(xi[:], bank[:, 0, :]).then_inc(gen_x_out, 1)
                    dve.wait_ge(gen_p_mm, n)

                def hot(k, n):
                    step(dve.tensor_scalar(rt[0:EP, T1, :], iota[0:EP, 0:NT], -float(P), float(P) + 1.0,
                                           ALU.mult, ALU.add))
                    step(dve.tensor_scalar(rt[0:EP, T1, :], rt[0:EP, T1, :], pair_f[0:EP, bass.ds(k, 1), 1], None, ALU.add))
                    dve.tensor_scalar(row_hot[0:EP, :], iota[0:EP, 0:P], shift[0:EP],
                                      pair_f[0:EP, bass.ds(k, 1), 0], ALU.add, ALU.is_equal)
                    dve.tensor_tensor(col_hot[0:EP, :].rearrange("p (t m) -> p t m", m=P),
                                      rt[0:EP, T1, :].rearrange("p (t o) -> p t o", o=1).broadcast_to((EP, NT, P)),
                                      iota[0:EP, 0:P].rearrange("p (o m) -> p o m", o=1).broadcast_to((EP, NT, P)),
                                      ALU.is_equal).then_inc(gen_hot, 1)

                dve.wait_ge(g_mm, NT)
                dve.wait_ge(g_out, NT - 1)
                dve.wait_ge(share_p, 2)
                dve.wait_ge(last_sym, 3)
                dve.memset(shift, -1.0)
                step(dve.memset(tile_no, 1.0))
                dve.sem_inc(gen_start, 1)
                w_out(1)
                dve.sem_inc(gen_k_out, 1)
                with dve.Fori(0, NT) as J:
                    x_out(J + 1)
                    dve.tensor_copy(kT[:, :, bass.ds(J * P, P)],
                                    bank[:, 1, :].rearrange("p (c e) -> p c e", c=DC)).then_inc(gen_k_out, 1)
                w_out(2)
                dve.sem_inc(gen_row, 1)
                with dve.Fori(0, NT) as I:
                    x_out(I + (NT + 1))
                    dve.tensor_copy(qT, bank[:, 1, :].rearrange("p (c e) -> p c e", c=DC)).then_inc(gen_q_out, 1)
                    hot(0, I)
                    with dve.Fori(1, EC) as k:
                        dve.wait_ge(gen_pair_mm, I * EC + k)
                        hot(k, I)
                    dve.wait_ge(gen_pair_mm, I * EC + EC)
                    step(dve.tensor_scalar(rt[:, T1, :], iota[:, 0:NT], tile_no, iota[:, P:P + 1],
                                           ALU.is_equal, ALU.mult))
                    step(dve.tensor_tensor(factor.rearrange("p (t m) -> p t m", m=P),
                                           rt[:, T1, :].rearrange("p (t o) -> p t o", o=1).broadcast_to((P, NT, P)),
                                           iota[:, 0:P].rearrange("p (o m) -> p o m", o=1).broadcast_to((P, NT, P)),
                                           ALU.is_equal))
                    step(dve.tensor_scalar(d_score, factor, -1.0, 1.0, ALU.mult, ALU.add))
                    dve.wait_ge(gen_a_in, I * 16 + 16)
                    step(dve.tensor_scalar(floor, fT, 1.0, -1.0, ALU.is_equal, ALU.add))
                    step(dve.scalar_tensor_tensor(floor, floor, BIG, d_score, ALU.mult, ALU.mult))
                    step(dve.scalar_tensor_tensor(floor, factor, SELF_SCORE, floor, ALU.mult, ALU.add))
                    dve.scalar_tensor_tensor(pair_mask, bank[:, 2:6, :].rearrange("p a b -> p (a b)"), 1.0, d_score,
                                             ALU.min, ALU.mult).then_inc(gen_masks, 1)
                    step(dve.memset(factor, 0.0))
                    for h in range(HEADS):
                        dve.wait_ge(gen_masks, I + 1)
                        dve.wait_ge(gen_s_mm, I * HEADS + (h + 1))
                        ins = dve.scalar_tensor_tensor(d_score, bank[:, 2:6, :].rearrange("p a b -> p (a b)"),
                                                       float(DK) ** -0.5, pair_mask, ALU.mult, ALU.mult)
                        ins.then_inc(gen_s_read, 1)
                        dve.wait_ge(gen_s_read, I * HEADS + (h + 1))
                        step(dve.tensor_tensor(d_score, d_score, floor, ALU.add))
                        step(dve.tensor_reduce(mv[:, 0, 0:1], d_score, AX, ALU.max))
                        dve.tensor_scalar(mv[:, 0, 1:2], mv[:, 0, 0:1], -1.0, None, ALU.mult).then_inc(gen_max, 1)
                        dve.wait_ge(gen_exp, I * HEADS + (h + 1))
                        step(dve.tensor_scalar(mv[:, 0, 3:4], mv[:, 0, 2:3], float(HEADS), None, ALU.mult))
                        step(dve.reciprocal(mv[:, 0, 3:4], mv[:, 0, 3:4]))
                        ins = dve.scalar_tensor_tensor(factor, d_score, mv[:, 0, 3:4], factor, ALU.mult, ALU.add)
                        if h < HEADS - 1:
                            step(ins)
                        else:
                            ins.then_inc(gen_factor, 1)
                    dve.wait_ge(gen_f_tr, I + 1)
                    dve.tensor_copy(fT, bank[:, 2:6, :].rearrange("p a b -> p (a b)")).then_inc(gen_f_out, 1)
                    dve.tensor_scalar(shift, shift, float(P), None, ALU.add)
                    step(dve.tensor_scalar(tile_no, tile_no, 1.0, None, ALU.add))
                    dve.wait_ge(gen_v_mm, I * 4 + 5)
                    dve.tensor_copy(g[:, bass.ds(I, 1), :], bank[:, 6:7, :]).then_inc(gen_row, 1)
                dve.memset(spare[:, 0:2 * N], 0.0)
                dve.memset(bank[:, 0:2, :], 0.0)
                dve.memset(bank[:, 7, :], 0.0)
                dve.wait_ge(gen_row, NT + 1)
                dve.tensor_copy(bank[:, 4 + (NT - 1) % 2, :], g[:, NT - 1, :])
                dve.memset(rt[:, ALPHA, :], 1.0)
                step(dve.memset(rt[:, BETA, :], 1.0))
                dve.wait_ge(gen_row, NT + 1)
                dve.sem_inc(gen_done, 1)

            with dve.If(dve.value_load(n_live[0:1, 0:1]) > P):
                general_path(dve)

            def moments(t, var_set):
                link(dve.bn_stats(stats[:, t % 2, :], g[:, t, :]))
                dve.bn_aggr(mv[:, t % 4, 0:2], stats[:, t % 2, :]).then_inc(var_set, 1)

            for t in range(NT + 1):
                now, prev = t < NT, 1 <= t <= NT
                m, mp = mv[:, t % 4, :], mv[:, (t - 1) % 4, :]
                if now:
                    dve.wait_ge(corr_mm, t + 1)
                    dve.wait_ge(g_out, t + 1)
                    y_at = mark(dve.scalar_tensor_tensor(g[:, t, :], g[:, t, :], rt[:, ALPHA, t:t + 1],
                                                         bank[:, (0, 1, 7)[t % 3], :], ALU.mult, ALU.add))
                if prev:
                    dve.wait_ge(root1, t)
                    s_at = mark(dve.reciprocal(mp[:, 4:5], mp[:, 3:4]))
                if now:
                    dve.wait_ge(xr_in[t % NXR], 16 * (t // NXR + 1))
                    dve.wait_ge(chain, y_at)
                    dve.scalar_tensor_tensor(g[:, t, :], x_again(t), rt[:, BETA, t:t + 1], g[:, t, :],
                                             ALU.mult, ALU.add).then_inc(x1_pre, 1)
                if prev:
                    dve.wait_ge(chain, s_at)
                    s_at = mark(dve.scalar_tensor_tensor(mp[:, 6:7], mp[:, 1:2], LN_EPS, mp[:, 4:5],
                                                         ALU.add, ALU.mult))
                    dve.wait_ge(chain, s_at)
                    s_at = mark(dve.scalar_tensor_tensor(mp[:, 6:7], mp[:, 6:7], -0.5, mp[:, 4:5],
                                                         ALU.mult, ALU.mult))
                if now:
                    dve.wait_ge(x1_pre, t + 1)
                    st_at = mark(dve.bn_stats(stats[:, t % 2, :], g[:, t, :]))
                if prev:
                    dve.wait_ge(chain, s_at)
                    s_at = mark(dve.scalar_tensor_tensor(mp[:, 4:5], mp[:, 6:7], 1.5, mp[:, 4:5],
                                                         ALU.add, ALU.mult))
                if now:
                    dve.wait_ge(chain, st_at)
                    dve.bn_aggr(m[:, 0:2], stats[:, t % 2, :]).then_inc(var1_set, 1)
                if prev:
                    dve.wait_ge(chain, s_at)
                    dve.scalar_tensor_tensor(mp[:, 5:6], mp[:, 0:1], -1.0, mp[:, 4:5],
                                             ALU.mult, ALU.mult).then_inc(norm1_set, 1)
            for t in range(NT):
                dve.wait_ge(vh_done, t + 1)
                dve.scalar_tensor_tensor(v_lo(t), bank[:, bank_of(t), :],
                                         rt[:, SCALE_V, t:t + 1], v_hi(t),
                                         ALU.mult, ALU.subtract).then_inc(vl_done, 1)
            for t in range(NT + 1):
                if t < NT:
                    dve.wait_ge(y_mm, t + 1)
                    dve.scalar_tensor_tensor(g[:, t, :], bank[:, bank_of(NT + t), :], 1.0 / V_SCALE, g[:, t, :],
                                             ALU.mult, ALU.add).then_inc(y_read, 1)
                    dve.wait_ge(y_read, t + 1)
                    if t >= 4:
                        dve.wait_ge(fin, t - 3)
                    moments(t, var2_set)
                if t:
                    m = mv[:, (t - 1) % 4, :]
                    dve.wait_ge(root2, t)
                    link(dve.reciprocal(m[:, 4:5], m[:, 3:4]))
                    link(dve.scalar_tensor_tensor(m[:, 6:7], m[:, 1:2], LN_EPS, m[:, 4:5], ALU.add, ALU.mult))
                    link(dve.scalar_tensor_tensor(m[:, 6:7], m[:, 6:7], -0.5, m[:, 4:5], ALU.mult, ALU.mult))
                    link(dve.scalar_tensor_tensor(m[:, 4:5], m[:, 6:7], 1.5, m[:, 4:5], ALU.add, ALU.mult))
                    dve.scalar_tensor_tensor(m[:, 5:6], m[:, 0:1], -1.0, m[:, 4:5],
                                             ALU.mult, ALU.mult).then_inc(fin_pre, 1)


def np_exp(v):
    import numpy as np
    return np.exp(np.float64(v))


_INS = ['x', 'adj', 'L0_gnn_rel_pair_index', 'L0_gnn_Wq', 'L0_gnn_bq', 'L0_gnn_Wk', 'L0_gnn_bk']


def kernel(**inputs):
    import numpy as _np
    import concourse.bacc as _bacc
    from concourse import mybir as _mybir
    from concourse.bass_utils import run_bass_kernel_spmd as _run

    nc = _bacc.Bacc("TRN2", target_bir_lowering=False, num_devices=1)
    arrays, args = {}, []
    for name in _INS:
        a = _np.ascontiguousarray(inputs[name])
        arrays[f"in_{name}_dram"] = a
        args.append(nc.dram_tensor(f"in_{name}_dram", a.shape, _mybir.dt.from_np(a.dtype), kind="ExternalInput").ap())
    args.append(nc.dram_tensor("out_dram", args[0].shape, _mybir.dt.float32, kind="ExternalOutput").ap())
    gnn_residual_kernel(nc, *args)
    r = _run(nc, [arrays], core_ids=[0])
    return r.results[0]["out_dram"]
```
